# Optimizing a Trainium2 kernel written in Bass

```python
import numpy as np
import jax
import jax.numpy as jnp

def _softmax(x, axis=-1):
    return jax.nn.softmax(x, axis=axis)

def _gelu(x):
    return jax.nn.gelu(x, approximate=True)

def _silu(x):
    return jax.nn.silu(x)

def _sigmoid(x):
    return jax.nn.sigmoid(x)

def _layernorm(x, axis=-1, eps=1e-05):
    m = jnp.mean(x, axis=axis, keepdims=True)
    v = jnp.var(x, axis=axis, keepdims=True)
    return (x - m) / jnp.sqrt(v + eps)

def _scatter_add(tgt, idx, src, axis=0):
    return tgt.at[idx].add(src)

def _segment_sum(src, seg, n):
    return jax.ops.segment_sum(src, seg, n)
kernel_name = 'mk_xattn_ffn_d1_seqx_r4_4c352e'

def setup_inputs(seed: int=0):
    np.random.seed(seed)
    _w = jnp.asarray

    def _rec_inputs():
        import jax
        import jax.numpy as jnp
        _rk = jax.random.key(seed)
        x = 7.22e-05 + 1 * jax.random.normal(jax.random.fold_in(_rk, 1), (4, 512, 512), jnp.float32)
        _lenS = 512 - jax.random.randint(jax.random.fold_in(_rk, 7), (4,), 0, max(1, 512 // 4) + 1, jnp.int32)
        _lenS2 = 512 - jax.random.randint(jax.random.fold_in(_rk, 8), (4,), 0, max(1, 512 // 4) + 1, jnp.int32)
        _ctx_1024P = jax.random.normal(jax.random.fold_in(_rk, 11), (4, 16, 256), jnp.float32)
        _ctx_1024c = jax.random.dirichlet(jax.random.fold_in(_rk, 511), 0.3 * jnp.ones((16,), jnp.float32), (4, 512))
        _ctx_1024t = jnp.einsum('bsk,bkd->bsd', _ctx_1024c, _ctx_1024P)
        _ctx_1024t = _ctx_1024t * jax.lax.rsqrt(jnp.mean(jnp.square(_ctx_1024t)) + 1e-12) * 0.953939
        ctx_1024 = 2.81802e-05 + 1.00001 * (_ctx_1024t + 0.3 * jax.random.normal(jax.random.fold_in(_rk, 611), (4, 512, 256), jnp.float32))
        return (x, ctx_1024)
    x, ctx_1024 = _rec_inputs()

    def _L0_xattn_setup():
        import jax, jax.numpy as jnp
        import numpy as np
        key = jax.random.key(seed)
        ks = jax.random.split(key, 6)
        B, L, N, C, D = (8, 128, 512, 256, 128)
        return {'teacher_logits': jax.random.normal(ks[0], (B, L, N), dtype=jnp.float32), 'teacher_features': jax.random.normal(ks[1], (B, N, C), dtype=jnp.float32), 'Wq': jax.random.normal(ks[2], (D, C), dtype=jnp.float32) * (1.0 / np.sqrt(C)), 'bq': jnp.zeros((D,), dtype=jnp.float32), 'Wk': jax.random.normal(ks[3], (D, C), dtype=jnp.float32) * (1.0 / np.sqrt(C)), 'bk': jnp.zeros((D,), dtype=jnp.float32)}
    _L0_xattn_all = _L0_xattn_setup()
    _L0_xattn_in = {k: v for k, v in _L0_xattn_all.items() if k in ('Wq', 'bq', 'Wk', 'bk')}
    del _L0_xattn_all

    def _L0_ffn_setup():
        import jax, jax.numpy as jnp
        import numpy as np
        DIM = 512
        N_EXPERTS = 8
        TOP_K = 2
        key = jax.random.key(seed)
        ks = jax.random.split(key, 5)
        x = jax.random.normal(ks[0], (4, 1024, DIM), dtype=jnp.float32)
        W_up = jax.random.normal(ks[1], (DIM, DIM), dtype=jnp.float32) * (1.0 / np.sqrt(DIM))
        W_down = jax.random.normal(ks[2], (DIM, DIM), dtype=jnp.float32) * (1.0 / np.sqrt(DIM))
        W_gate = jax.random.normal(ks[3], (N_EXPERTS, DIM), dtype=jnp.float32) * (1.0 / np.sqrt(DIM))
        W_expert = jax.random.normal(ks[4], (DIM, DIM), dtype=jnp.float32) * (1.0 / np.sqrt(DIM))
        return {'x': x, 'W_up': W_up, 'W_down': W_down, 'W_gate': W_gate, 'W_expert': W_expert}
    _L0_ffn_all = _L0_ffn_setup()
    _L0_ffn_in = {k: v for k, v in _L0_ffn_all.items() if k in ('W_up', 'W_down', 'W_gate', 'W_expert')}
    del _L0_ffn_all
    return {'x': x, 'ctx_1024': ctx_1024, 'L0_xattn_Wq': _L0_xattn_in['Wq'], 'L0_xattn_bq': _L0_xattn_in['bq'], 'L0_xattn_Wk': _L0_xattn_in['Wk'], 'L0_xattn_bk': _L0_xattn_in['bk'], 'L0_ffn_W_up': _L0_ffn_in['W_up'], 'L0_ffn_W_down': _L0_ffn_in['W_down'], 'L0_ffn_W_gate': _L0_ffn_in['W_gate'], 'L0_ffn_W_expert': _L0_ffn_in['W_expert']}

def reference(x, ctx_1024, L0_xattn_Wq, L0_xattn_bq, L0_xattn_Wk, L0_xattn_bk, L0_ffn_W_up, L0_ffn_W_down, L0_ffn_W_gate, L0_ffn_W_expert):
    import jax
    import jax.numpy as jnp

    def _L0_xattn_ref(teacher_logits, teacher_features, Wq, bq, Wk, bk):
        import jax, jax.numpy as jnp
        import numpy as np
        query = jnp.einsum('bnc,dc->bnd', teacher_features, Wq) + bq
        key = jnp.einsum('bnc,dc->bnd', teacher_features, Wk) + bk
        energy = jnp.einsum('bnd,bmd->bnm', query, key)
        attention = jax.nn.softmax(energy, axis=-1)
        x_m = jnp.einsum('bln,bmn->blm', teacher_logits, attention)
        return x_m

    def _L0_ffn_ref(x, W_up, W_down, W_gate, W_expert):
        import jax, jax.numpy as jnp
        import numpy as np
        DIM = 512
        N_EXPERTS = 8
        TOP_K = 2
        logits = jnp.einsum('bsd,ed->bse', x, W_gate)
        routing_weights, selected_experts = jax.lax.top_k(logits, TOP_K)
        shared_out = jnp.einsum('bsd,od->bso', jax.nn.relu(jnp.einsum('bsd,od->bso', x, W_up)), W_down)
        rw = jax.nn.softmax(routing_weights, axis=-1)
        expert_out = jnp.einsum('bsd,do->bso', x, W_expert)
        moe_out = jnp.sum(rw, axis=-1, keepdims=True) * expert_out
        return shared_out + moe_out
    x = x + _L0_xattn_ref(_layernorm(x, axis=-1), ctx_1024, L0_xattn_Wq, L0_xattn_bq, L0_xattn_Wk, L0_xattn_bk)
    x = x + _L0_ffn_ref(_layernorm(x, axis=-1), L0_ffn_W_up, L0_ffn_W_down, L0_ffn_W_gate, L0_ffn_W_expert)
    return x

_drawn_inputs = setup_inputs


def setup_inputs(seed=0):
    import zlib

    import numpy as np

    out = dict(_drawn_inputs(seed))
    spreads = {'L0_xattn_bq': (0.0, 0.1), 'L0_xattn_bk': (0.0, 0.1)}
    factors = {}
    for name, (base, spread) in spreads.items():
        noise = np.random.default_rng([zlib.crc32(name.encode()), seed]).standard_normal(out[name].shape)
        drawn = base * np.exp(spread * noise) if base else spread * noise
        out[name] = jnp.asarray(drawn.astype(out[name].dtype))
    for name, factor in factors.items():
        out[name] = (out[name] * factor).astype(out[name].dtype)
    return out
```

```python
from contextlib import ExitStack

import concourse.bass as bass
from concourse import mybir

ALU = mybir.AluOpType
ACT = mybir.ActivationFunctionType
AX = mybir.AxisListType
F32 = mybir.dt.float32
PART = mybir.dt.float16

P = 128
W_SCALE = 2.0**4
A_SCALE = 2.0**10
EPS = 1e-5


def build(nc, x, xT, ctxT, WqkT, bqk, WupT, WdownT, Wexpert, WgateT, out):
    B, _, LT, D = x.shape
    KT = D // P
    L = LT * P
    CT = ctxT.shape[2]
    H = WqkT.shape[3]
    E = WgateT.shape[2]
    assert D == L and H == P and E == 8

    es = ExitStack()

    def sb(name, shape, dt=F32):
        return es.enter_context(nc.sbuf_tensor(name, shape, dt))

    def bank(name):
        return es.enter_context(nc.psum_tensor(name, [P, 512], F32))

    def sem(name):
        return es.enter_context(nc.semaphore(name))

    with es:
        x_sb = sb("x_sb", [P, LT, D])
        xT_sb = sb("xT_sb", [P, KT, L])
        xT_hi = sb("xT_hi", [P, KT, L], PART)
        xT_lo = sb("xT_lo", [P, KT, L], PART)
        ctx_sb = sb("ctx_sb", [P, CT, L])
        ctx_hi = sb("ctx_hi", [P, CT, L], PART)
        ctx_lo = sb("ctx_lo", [P, CT, L], PART)
        qk_hi = sb("qk_hi", [P, 2, L], PART)
        qk_lo = sb("qk_lo", [P, 2, L], PART)
        attn = sb("attn", [P, KT, D])
        attnT_hi = sb("attnT_hi", [P, KT, D], PART)
        attnT_lo = sb("attnT_lo", [P, KT, D], PART)
        x2 = sb("x2", [P, LT, D])
        y = sb("y", [P, LT, D])
        yT_hi = sb("yT_hi", [P, KT, L], PART)
        yT_lo = sb("yT_lo", [P, KT, L], PART)
        hT_hi = sb("hT_hi", [P, KT, L], PART)
        hT_lo = sb("hT_lo", [P, KT, L], PART)
        base = sb("base", [P, LT, D])
        out_sb = sb("out_sb", [P, LT, D])

        wqk = sb("wqk", [P, CT, 2, H])
        wqk_hi = sb("wqk_hi", [P, CT, 2, H], PART)
        wqk_lo = sb("wqk_lo", [P, CT, 2, H], PART)
        bias = sb("bias", [P, 2])
        bias_scaled = sb("bias_scaled", [P, 2])
        wgate = sb("wgate", [P, KT, E])
        wgate_hl = sb("wgate_hl", [P, KT, 2, E], PART)
        wexp = sb("wexp", [P, KT, D])
        wexp_hi = sb("wexp_hi", [P, KT, D], PART)
        wexp_lo = sb("wexp_lo", [P, KT, D], PART)
        wup = sb("wup", [P, KT, D])
        wup_hi = sb("wup_hi", [P, KT, D], PART)
        wup_lo = sb("wup_lo", [P, KT, D], PART)
        wdown = sb("wdown", [P, KT, D])
        wdown_hi = sb("wdown_hi", [P, KT, D], PART)
        wdown_lo = sb("wdown_lo", [P, KT, D], PART)

        identity = sb("identity", [P, P])
        minus_half = sb("minus_half", [P, LT])
        neg_max = sb("neg_max", [P, KT])
        row_max = sb("row_max", [P, KT])
        row_sum = sb("row_sum", [P, KT])
        row_scale = sb("row_scale", [P, KT])
        row_mean = sb("row_mean", [P, KT])
        stats1 = sb("stats1", [P, LT, 6])
        mean_var1 = sb("mean_var1", [P, LT, 2])
        var1 = sb("var1", [P, LT])
        rstd1 = sb("rstd1", [P, LT])
        stats2 = sb("stats2", [P, LT, 6])
        mean_var2 = sb("mean_var2", [P, LT, 2])
        mean2 = sb("mean2", [P, LT])
        var2 = sb("var2", [P, LT])
        rstd2 = sb("rstd2", [P, LT])
        logits = sb("logits", [P, LT, E])
        top = sb("top", [P, LT, 8])
        top_one = sb("top_one", [P, LT])
        neg_top = sb("neg_top", [P, LT])
        top_exp = sb("top_exp", [P, LT, 2])
        top_sum = sb("top_sum", [P, LT])
        top_inv = sb("top_inv", [P, LT])
        top_prob = sb("top_prob", [P, LT, 2])
        route = sb("route", [P, LT])

        small = [bank("small0"), bank("small1")]
        turned = [bank("turned0"), bank("turned1")]
        big = [bank(f"big{i}") for i in range(4)]

        ctx_in, x_in, xT_in = sem("ctx_in"), sem("x_in"), sem("xT_in")
        wqk_in, wexp_in, wup_in, wdown_in = sem("wqk_in"), sem("wexp_in"), sem("wup_in"), sem("wdown_in")
        out_stored = [sem(f"out_stored{t}") for t in range(LT)]
        identity_ready = sem("identity_ready")
        wqk_hi_ready, wqk_split = sem("wqk_hi_ready"), sem("wqk_split")
        wexp_hi_ready, wexp_split = sem("wexp_hi_ready"), sem("wexp_split")
        wup_hi_ready, wup_split = sem("wup_hi_ready"), sem("wup_split")
        wdown_hi_ready, wdown_split = sem("wdown_hi_ready"), sem("wdown_split")
        ctx_hi_ready, ctx_split = sem("ctx_hi_ready"), sem("ctx_split")
        xT_hi_ready, xT_split = sem("xT_hi_ready"), sem("xT_split")
        proj_ready = sem("proj_ready")
        qk_hi_ready, qk_split = sem("qk_hi_ready"), sem("qk_split")
        energy_ready = sem("energy_ready")
        max_ready, neg_max_ready = sem("max_ready"), sem("neg_max_ready")
        exp_ready = sem("exp_ready")
        row_scale_ready, row_mean_ready = sem("row_scale_ready"), sem("row_mean_ready")
        attn_ready = sem("attn_ready")
        turned_ready, turned_hi_ready, turned_split = sem("turned_ready"), sem("turned_hi_ready"), sem("turned_split")
        stats1_ready, mean1_ready, var1_ready, rstd1_ready = (
            sem("stats1_ready"), sem("mean1_ready"), sem("var1_ready"), sem("rstd1_ready"))
        mix_ready = sem("mix_ready")
        x2_ready, stats2_ready, mean2_ready = sem("x2_ready"), sem("stats2_ready"), sem("mean2_ready")
        var2_ready, rstd2_ready, y_ready = sem("var2_ready"), sem("rstd2_ready"), sem("y_ready")
        gate_ready, logits_ready, top_ready, neg_top_ready = (
            sem("gate_ready"), sem("logits_ready"), sem("top_ready"), sem("neg_top_ready"))
        top_exp_ready, top_inv_ready, top_prob_ready, route_ready = (
            sem("top_exp_ready"), sem("top_inv_ready"), sem("top_prob_ready"), sem("route_ready"))
        expert_ready, base_ready = sem("expert_ready"), sem("base_ready")
        up_ready, hT_hi_ready, hT_split = sem("up_ready"), sem("hT_hi_ready"), sem("hT_split")
        down_ready, out_ready = sem("down_ready"), sem("out_ready")

        block = es.enter_context(nc.Block())

        def over_batches(eng, body):
            body(0, True, False)
            with eng.Fori(1, B - 1) as b:
                body(b, False, False)
            body(B - 1, False, True)

        @block.sync
        def _(sp):
            sp.dma_start(ctx_sb[:], ctxT[0]).then_inc(ctx_in, 16)
            sp.dma_start(wqk[:], WqkT).then_inc(wqk_in, 16)
            sp.dma_start(bias[:], bqk).then_inc(wqk_in, 16)
            sp.dma_start(xT_sb[:], xT[0]).then_inc(xT_in, 16)
            sp.dma_start(x_sb[:], x[0]).then_inc(x_in, 16)
            sp.dma_start(wexp[:], Wexpert).then_inc(wexp_in, 16)
            sp.dma_start(wgate[:], WgateT).then_inc(wexp_in, 16)
            sp.dma_start(wup[:], WupT).then_inc(wup_in, 16)
            sp.dma_start(wdown[:], WdownT).then_inc(wdown_in, 16)

            def body(b, first, last):
                if not last:
                    sp.wait_ge(ctx_split, b + 1)
                    sp.dma_start(ctx_sb[:], ctxT[b + 1]).then_inc(ctx_in, 16)
                    sp.wait_ge(xT_split, b + 1)
                    sp.dma_start(xT_sb[:], xT[b + 1]).then_inc(xT_in, 16)
                    sp.wait_ge(x2_ready, b * LT + LT)
                    sp.dma_start(x_sb[:], x[b + 1]).then_inc(x_in, 16)
                for t in range(LT):
                    sp.wait_ge(out_ready, b * LT + t + 1)
                    sp.dma_start(out[b, :, t, :], out_sb[:, t, :]).then_inc(out_stored[t], 16)

            over_batches(sp, body)
            for t in range(LT):
                sp.wait_ge(out_stored[t], B * 16)

        @block.tensor
        def _(pe):
            def product(bank_out, lhs_hi, lhs_lo, rhs_hi, rhs_lo, n):
                for k in range(n):
                    pe.matmul(bank_out, lhs_hi(k), rhs_hi(k), start=(k == 0), stop=False)
                    pe.matmul(bank_out, lhs_hi(k), rhs_lo(k), start=False, stop=False)
                    mm = pe.matmul(bank_out, lhs_lo(k), rhs_hi(k), start=False, stop=(k == n - 1))
                return mm

            def project(b):
                pe.wait_ge(ctx_split, b + 1)
                for i in range(2):
                    product(small[1 - i][:], lambda c: wqk_hi[:, c, i, :], lambda c: wqk_lo[:, c, i, :],
                            lambda c: ctx_hi[:, c, :], lambda c: ctx_lo[:, c, :], CT).then_inc(proj_ready, 1)

            def energies(b, tiles):
                for m in tiles:
                    if m == 0:
                        pe.wait_ge(qk_split, b * 2 + 2)
                    if m >= 2:
                        pe.wait_ge(exp_ready, b * KT + m - 1)
                    rows = slice(m * P, m * P + P)
                    product(small[m % 2][:], lambda k: qk_hi[:, 0, rows], lambda k: qk_lo[:, 0, rows],
                            lambda k: qk_hi[:, 1, :], lambda k: qk_lo[:, 1, :], 1).then_inc(energy_ready, 1)

            def turn(n, src):
                for k in range(KT):
                    mm = pe.transpose(turned[n % 2][:, k * P:(k + 1) * P], src[:, k * P:(k + 1) * P], identity[:])
                mm.then_inc(turned_ready, 1)

            def turn_attn(b, tiles, first=False):
                for m in tiles:
                    if m >= 2 or not first:
                        pe.wait_ge(turned_split, b * (KT + LT) + m - 1)
                    pe.wait_ge(attn_ready, b * KT + m + 1)
                    turn(m, attn[:, m, :])

            def turn_y(b, t):
                pe.wait_ge(turned_split, b * (KT + LT) + KT + t - 1)
                pe.wait_ge(y_ready, b * LT + t + 1)
                turn(KT + t, y[:, t, :])

            def mix(b, t, first):
                if t == 0:
                    pe.wait_ge(turned_split, b * (KT + LT) + KT)
                    pe.wait_ge(xT_split, b + 1)
                if not first:
                    pe.wait_ge(out_ready, b * LT + t + 1 - LT)
                rows = slice(t * P, t * P + P)
                product(big[t][:], lambda k: xT_hi[:, k, rows], lambda k: xT_lo[:, k, rows],
                        lambda k: attnT_hi[:, k, :], lambda k: attnT_lo[:, k, :], KT).then_inc(mix_ready, 1)

            def expert(b, t, first):
                if first and t == 0:
                    pe.wait_ge(wexp_split, 2)
                pe.wait_ge(turned_split, b * (KT + LT) + KT + t + 1)
                if t >= 1:
                    pe.wait_ge(logits_ready, b * LT + t)
                rows = slice(t * P, t * P + P)
                g = small[0][:, 0:2 * E]
                for k in range(KT):
                    pe.matmul(g, yT_hi[:, k, rows], wgate_hl[:, k, :, :].rearrange("p a e -> p (a e)"),
                              start=(k == 0), stop=False)
                    mm = pe.matmul(g[:, 0:E], yT_lo[:, k, rows], wgate_hl[:, k, 0, :],
                                   start=False, stop=(k == KT - 1))
                mm.then_inc(gate_ready, 1)
                pe.wait_ge(x2_ready, b * LT + t + 1)
                product(big[t][:], lambda k: yT_hi[:, k, rows], lambda k: yT_lo[:, k, rows],
                        lambda k: wexp_hi[:, k, :], lambda k: wexp_lo[:, k, :], KT).then_inc(expert_ready, 1)

            def up(b, f, first):
                if first and f == 0:
                    pe.wait_ge(wup_split, 1)
                pe.wait_ge(base_ready, b * LT + f + 1)
                rows = slice(f * P, f * P + P)
                product(big[f][:], lambda k: wup_hi[:, k, rows], lambda k: wup_lo[:, k, rows],
                        lambda k: yT_hi[:, k, :], lambda k: yT_lo[:, k, :], KT).then_inc(up_ready, 1)

            def down(b, t, first):
                if first and t == 0:
                    pe.wait_ge(wdown_split, 1)
                if t == 0:
                    pe.wait_ge(hT_split, b * KT + KT)
                rows = slice(t * P, t * P + P)
                product(big[t][:], lambda k: hT_hi[:, k, rows], lambda k: hT_lo[:, k, rows],
                        lambda k: wdown_hi[:, k, :], lambda k: wdown_lo[:, k, :], KT).then_inc(down_ready, 1)

            pe.wait_ge(wqk_split, 1)
            project(0)
            energies(0, range(KT))
            pe.wait_ge(identity_ready, 2)
            turn_attn(0, range(KT), first=True)

            def body(b, first, last):
                mix(b, 0, first)
                mix(b, 1, first)
                mix(b, 2, first)
                turn_y(b, 0)
                mix(b, 3, first)
                turn_y(b, 1)
                expert(b, 0, first)
                turn_y(b, 2)
                expert(b, 1, first)
                turn_y(b, 3)
                expert(b, 2, first)
                expert(b, 3, first)
                if not last:
                    pe.wait_ge(logits_ready, b * LT + LT)
                    project(b + 1)
                up(b, 0, first)
                up(b, 1, first)
                up(b, 2, first)
                if not last:
                    energies(b + 1, (0, 1))
                up(b, 3, first)
                if not last:
                    energies(b + 1, (2, 3))
                down(b, 0, first)
                down(b, 1, first)
                if not last:
                    turn_attn(b + 1, (0, 1))
                down(b, 2, first)
                if not last:
                    turn_attn(b + 1, (2, 3))
                down(b, 3, first)

            over_batches(pe, body)

        @block.scalar
        def _(act):
            def qk_high(b):
                for i in range(2):
                    act.wait_ge(proj_ready, b * 2 + i + 1)
                    nc.scalar.activation(qk_hi[:, i, :], small[1 - i][:], ACT.Identity,
                                         bias=bias_scaled[:, i:i + 1]).then_inc(qk_hi_ready, 1)

            def exps(b, tiles):
                for m in tiles:
                    act.wait_ge(neg_max_ready, b * KT + m + 1)
                    nc.scalar.activation(attn[:, m, :], small[m % 2][:], ACT.Exp, bias=neg_max[:, m:m + 1],
                                         scale=1 / W_SCALE**2, accum_out=row_sum[:, m:m + 1]).then_inc(exp_ready, 1)

            def turned_high(b, n, to, t):
                act.wait_ge(turned_ready, b * (KT + LT) + n + 1)
                nc.scalar.copy(to[:, :, t * P:(t + 1) * P],
                               turned[n % 2][:].rearrange("p (k c) -> p k c", k=KT)).then_inc(turned_hi_ready, 1)

            def gate_exp(b, t):
                act.wait_ge(neg_top_ready, b * LT + t + 1)
                nc.scalar.activation(top_exp[:, t, :], top[:, t, 0:2], ACT.Exp, bias=neg_top[:, t:t + 1],
                                     scale=1 / W_SCALE, accum_out=top_sum[:, t:t + 1]).then_inc(top_exp_ready, 1)

            def relu_high(b, f):
                act.wait_ge(up_ready, b * KT + f + 1)
                nc.scalar.activation(hT_hi[:, f, :], big[f][:], ACT.Relu).then_inc(hT_hi_ready, 1)

            def weight_high(arrived, n, hi, w, ready):
                act.wait_ge(arrived, n)
                nc.scalar.mul(hi, w, W_SCALE).then_inc(ready, 1)

            weight_high(wqk_in, 32, wqk_hi[:], wqk[:], wqk_hi_ready)
            nc.scalar.mul(bias_scaled[:], bias[:], W_SCALE).then_inc(wqk_hi_ready, 1)
            act.wait_ge(wqk_hi_ready, 2)
            qk_high(0)
            exps(0, range(KT))
            weight_high(wexp_in, 32, wexp_hi[:], wexp[:], wexp_hi_ready)
            nc.scalar.mul(wgate_hl[:, :, 0, :], wgate[:], W_SCALE).then_inc(wexp_hi_ready, 1)
            for m in range(KT):
                turned_high(0, m, attnT_hi, m)

            def body(b, first, last):
                if first:
                    weight_high(wup_in, 16, wup_hi[:], wup[:], wup_hi_ready)
                turned_high(b, KT + 0, yT_hi, 0)
                turned_high(b, KT + 1, yT_hi, 1)
                gate_exp(b, 0)
                turned_high(b, KT + 2, yT_hi, 2)
                gate_exp(b, 1)
                turned_high(b, KT + 3, yT_hi, 3)
                gate_exp(b, 2)
                gate_exp(b, 3)
                if first:
                    weight_high(wdown_in, 16, wdown_hi[:], wdown[:], wdown_hi_ready)
                if not last:
                    qk_high(b + 1)
                relu_high(b, 0)
                relu_high(b, 1)
                relu_high(b, 2)
                if not last:
                    exps(b + 1, (0, 1))
                relu_high(b, 3)
                if not last:
                    exps(b + 1, (2, 3))
                    for m in range(KT):
                        turned_high(b + 1, m, attnT_hi, m)

            over_batches(act, body)

        @block.vector
        def _(dve):
            def weight_low(hi_ready, n, lo, w, hi, ready):
                dve.wait_ge(hi_ready, n)
                nc.vector.scalar_tensor_tensor(out=lo, in0=w, scalar=W_SCALE, in1=hi,
                                               op0=ALU.mult, op1=ALU.subtract).then_inc(ready, 1)

            def ctx_high(b):
                dve.wait_ge(ctx_in, b * 16 + 16)
                if not isinstance(b, int) or b > 0:
                    dve.wait_ge(proj_ready, b * 2)
                nc.vector.tensor_copy(ctx_hi[:], ctx_sb[:]).then_inc(ctx_hi_ready, 1)

            def xT_high(b):
                dve.wait_ge(xT_in, b * 16 + 16)
                nc.vector.tensor_copy(xT_hi[:], xT_sb[:]).then_inc(xT_hi_ready, 1)

            def qk_low(b):
                for i in range(2):
                    dve.wait_ge(qk_hi_ready, b * 2 + i + 1)
                    nc.vector.scalar_tensor_tensor(out=qk_lo[:, i, :], in0=small[1 - i][:], scalar=bias_scaled[:, i:i + 1],
                                                   in1=qk_hi[:, i, :], op0=ALU.add, op1=ALU.subtract).then_inc(qk_split, 1)

            def maxima(b, tiles):
                for m in tiles:
                    dve.wait_ge(energy_ready, b * KT + m + 1)
                    nc.vector.tensor_reduce(row_max[:, m:m + 1], small[m % 2][:], AX.X, ALU.max).then_inc(max_ready, 1)
                    dve.wait_ge(max_ready, b * KT + m + 1)
                    nc.vector.tensor_scalar(neg_max[:, m:m + 1], row_max[:, m:m + 1], -1 / W_SCALE**2, None,
                                            ALU.mult).then_inc(neg_max_ready, 1)

            def normalize(b, tiles):
                for m in tiles:
                    dve.wait_ge(exp_ready, b * KT + m + 1)
                    nc.vector.reciprocal(row_scale[:, m:m + 1], row_sum[:, m:m + 1]).then_inc(row_scale_ready, 1)
                    dve.wait_ge(row_scale_ready, b * KT * 2 + 2 * m + 1)
                    nc.vector.tensor_scalar(row_scale[:, m:m + 1], row_scale[:, m:m + 1], A_SCALE, None,
                                            ALU.mult).then_inc(row_scale_ready, 1)
                    dve.wait_ge(row_scale_ready, b * KT * 2 + 2 * m + 2)
                    nc.vector.tensor_scalar(row_mean[:, m:m + 1], row_sum[:, m:m + 1], row_scale[:, m:m + 1], 1.0 / D,
                                            ALU.mult, ALU.mult).then_inc(row_mean_ready, 1)
                    dve.wait_ge(row_mean_ready, b * KT + m + 1)
                    nc.vector.tensor_scalar(attn[:, m, :], attn[:, m, :], row_scale[:, m:m + 1], row_mean[:, m:m + 1],
                                            ALU.mult, ALU.subtract).then_inc(attn_ready, 1)

            def turned_low(b, n, hi, lo, t):
                dve.wait_ge(turned_hi_ready, b * (KT + LT) + n + 1)
                cols = slice(t * P, (t + 1) * P)
                nc.vector.tensor_tensor(lo[:, :, cols], turned[n % 2][:].rearrange("p (k c) -> p k c", k=KT),
                                        hi[:, :, cols], ALU.subtract).then_inc(turned_split, 1)

            def variance1(b):
                dve.wait_ge(x_in, b * 16 + 16)
                nc.vector.bn_stats(stats1[:, 0, :], x_sb[:, 0, :]).then_inc(stats1_ready, 1)
                for t in range(1, LT):
                    dve.wait_ge(stats1_ready, b * LT + t)
                    nc.vector.bn_stats(stats1[:, t, :], x_sb[:, t, :]).then_inc(stats1_ready, 1)
                    nc.vector.bn_aggr(mean_var1[:, t - 1, :], stats1[:, t - 1, :]).then_inc(mean1_ready, 1)
                dve.wait_ge(stats1_ready, b * LT + LT)
                dve.wait_ge(mean1_ready, b * LT + LT - 1)
                nc.vector.tensor_scalar(var1[:, 0:LT - 1], mean_var1[:, 0:LT - 1, 1], EPS, A_SCALE**2,
                                        ALU.add, ALU.mult).then_inc(var1_ready, 1)
                nc.vector.bn_aggr(mean_var1[:, LT - 1, :], stats1[:, LT - 1, :]).then_inc(mean1_ready, 1)
                dve.wait_ge(mean1_ready, b * LT + LT)
                nc.vector.tensor_scalar(var1[:, LT - 1:LT], mean_var1[:, LT - 1, 1:2], EPS, A_SCALE**2,
                                        ALU.add, ALU.mult).then_inc(var1_ready, 1)

            def residual(b, t):
                dve.wait_ge(mix_ready, b * LT + t + 1)
                if t == 0:
                    dve.wait_ge(rstd1_ready, b + 1)
                nc.vector.scalar_tensor_tensor(out=x2[:, t, :], in0=big[t][:], scalar=rstd1[:, t:t + 1], in1=x_sb[:, t, :],
                                               op0=ALU.mult, op1=ALU.add).then_inc(x2_ready, 1)
                dve.wait_ge(x2_ready, b * LT + t + 1)
                nc.vector.bn_stats(stats2[:, t, :], x2[:, t, :]).then_inc(stats2_ready, 1)
                dve.wait_ge(stats2_ready, b * LT + t + 1)
                nc.vector.tensor_scalar(mean2[:, t:t + 1], stats2[:, t, 1:2], stats2[:, t, 4:5], 0.5,
                                        ALU.add, ALU.mult).then_inc(mean2_ready, 1)
                nc.vector.bn_aggr(mean_var2[:, t, :], stats2[:, t, :]).then_inc(mean2_ready, 1)
                dve.wait_ge(mean2_ready, (b * LT + t + 1) * 2)
                nc.vector.tensor_scalar(var2[:, t:t + 1], mean_var2[:, t, 1:2], EPS, None, ALU.add).then_inc(var2_ready, 1)

            def norm_y(b, t):
                dve.wait_ge(rstd2_ready, b * LT + t + 1)
                nc.vector.tensor_scalar(y[:, t, :], x2[:, t, :], mean2[:, t:t + 1], rstd2[:, t:t + 1],
                                        ALU.subtract, ALU.mult).then_inc(y_ready, 1)

            def gate(b, t):
                dve.wait_ge(gate_ready, b * LT + t + 1)
                nc.vector.tensor_reduce(logits[:, t, :], small[0][:, 0:2 * E].rearrange("p (a e) -> p e a", a=2),
                                        AX.X, ALU.add).then_inc(logits_ready, 1)
                dve.wait_ge(logits_ready, b * LT + t + 1)
                nc.vector.tensor_reduce(top_one[:, t:t + 1], logits[:, t, :], AX.X, ALU.max).then_inc(top_ready, 1)
                nc.vector.max(top[:, t, :], logits[:, t, :]).then_inc(top_ready, 1)
                dve.wait_ge(top_ready, (b * LT + t + 1) * 2)
                nc.vector.tensor_scalar(neg_top[:, t:t + 1], top_one[:, t:t + 1], -1 / W_SCALE, None,
                                        ALU.mult).then_inc(neg_top_ready, 1)

            def routed(b, t):
                dve.wait_ge(top_exp_ready, b * LT + t + 1)
                nc.vector.reciprocal(top_inv[:, t:t + 1], top_sum[:, t:t + 1]).then_inc(top_inv_ready, 1)
                dve.wait_ge(top_inv_ready, b * LT + t + 1)
                nc.vector.tensor_scalar(top_prob[:, t, :], top_exp[:, t, :], top_inv[:, t:t + 1], 1 / W_SCALE,
                                        ALU.mult, ALU.mult).then_inc(top_prob_ready, 1)
                dve.wait_ge(top_prob_ready, b * LT + t + 1)
                nc.vector.tensor_reduce(route[:, t:t + 1], top_prob[:, t, :], AX.X, ALU.add).then_inc(route_ready, 1)
                dve.wait_ge(route_ready, b * LT + t + 1)
                dve.wait_ge(expert_ready, b * LT + t + 1)
                nc.vector.scalar_tensor_tensor(out=base[:, t, :], in0=big[t][:], scalar=route[:, t:t + 1], in1=x2[:, t, :],
                                               op0=ALU.mult, op1=ALU.add).then_inc(base_ready, 1)

            def relu_low(b, f):
                dve.wait_ge(hT_hi_ready, b * KT + f + 1)
                nc.vector.scalar_tensor_tensor(out=hT_lo[:, f, :], in0=big[f][:], scalar=0.0, in1=hT_hi[:, f, :],
                                               op0=ALU.max, op1=ALU.subtract).then_inc(hT_split, 1)

            def finish(b, t):
                dve.wait_ge(down_ready, b * LT + t + 1)
                if not isinstance(b, int) or b > 0:
                    dve.wait_ge(out_stored[t], b * 16)
                nc.vector.scalar_tensor_tensor(out=out_sb[:, t, :], in0=big[t][:], scalar=1 / W_SCALE**2, in1=base[:, t, :],
                                               op0=ALU.mult, op1=ALU.add).then_inc(out_ready, 1)

            ctx_high(0)
            weight_low(wqk_hi_ready, 2, wqk_lo[:], wqk[:], wqk_hi[:], wqk_split)
            xT_high(0)
            qk_low(0)
            variance1(0)
            maxima(0, (0, 1))
            normalize(0, (0, 1))
            maxima(0, (2, 3))
            normalize(0, (2, 3))
            for m in range(KT):
                turned_low(0, m, attnT_hi, attnT_lo, m)
            weight_low(wexp_hi_ready, 2, wexp_lo[:], wexp[:], wexp_hi[:], wexp_split)
            weight_low(wexp_hi_ready, 2, wgate_hl[:, :, 1, :], wgate[:], wgate_hl[:, :, 0, :], wexp_split)

            def body(b, first, last):
                residual(b, 0)
                residual(b, 1)
                norm_y(b, 0)
                residual(b, 2)
                norm_y(b, 1)
                turned_low(b, KT + 0, yT_hi, yT_lo, 0)
                residual(b, 3)
                norm_y(b, 2)
                turned_low(b, KT + 1, yT_hi, yT_lo, 1)
                norm_y(b, 3)
                gate(b, 0)
                turned_low(b, KT + 2, yT_hi, yT_lo, 2)
                if first:
                    weight_low(wup_hi_ready, 1, wup_lo[:], wup[:], wup_hi[:], wup_split)
                if not last:
                    ctx_high(b + 1)
                routed(b, 0)
                gate(b, 1)
                turned_low(b, KT + 3, yT_hi, yT_lo, 3)
                routed(b, 1)
                gate(b, 2)
                routed(b, 2)
                gate(b, 3)
                routed(b, 3)
                if not last:
                    qk_low(b + 1)
                if first:
                    weight_low(wdown_hi_ready, 1, wdown_lo[:], wdown[:], wdown_hi[:], wdown_split)
                relu_low(b, 0)
                if not last:
                    variance1(b + 1)
                relu_low(b, 1)
                if not last:
                    xT_high(b + 1)
                relu_low(b, 2)
                if not last:
                    maxima(b + 1, (0, 1))
                    normalize(b + 1, (0, 1))
                relu_low(b, 3)
                if not last:
                    maxima(b + 1, (2, 3))
                    normalize(b + 1, (2, 3))
                finish(b, 0)
                finish(b, 1)
                if not last:
                    turned_low(b + 1, 0, attnT_hi, attnT_lo, 0)
                    turned_low(b + 1, 1, attnT_hi, attnT_lo, 1)
                finish(b, 2)
                if not last:
                    turned_low(b + 1, 2, attnT_hi, attnT_lo, 2)
                    turned_low(b + 1, 3, attnT_hi, attnT_lo, 3)
                finish(b, 3)

            over_batches(dve, body)

        @block.gpsimd
        def _(pool):
            nc.gpsimd.memset(identity[:], 0.0).then_inc(identity_ready, 1)
            pool.wait_ge(identity_ready, 1)
            nc.gpsimd.affine_select(out=identity[:], in_=identity[:], compare_op=ALU.not_equal, fill=1.0, base=0,
                                    pattern=[[-1, P]], channel_multiplier=1).then_inc(identity_ready, 1)
            nc.gpsimd.memset(minus_half[:], -0.5).then_inc(identity_ready, 1)
            pool.wait_ge(identity_ready, 3)

            def ctx_low(b):
                pool.wait_ge(ctx_hi_ready, b + 1)
                nc.gpsimd.tensor_tensor(ctx_lo[:], ctx_sb[:], ctx_hi[:], ALU.subtract).then_inc(ctx_split, 1)

            def xT_low(b):
                pool.wait_ge(xT_hi_ready, b + 1)
                nc.gpsimd.tensor_tensor(xT_lo[:], xT_sb[:], xT_hi[:], ALU.subtract).then_inc(xT_split, 1)

            def power1(b):
                pool.wait_ge(var1_ready, b * 2 + 2)
                nc.gpsimd.tensor_tensor(rstd1[:], var1[:], minus_half[:], ALU.pow).then_inc(rstd1_ready, 1)

            def power2(b, t):
                pool.wait_ge(var2_ready, b * LT + t + 1)
                nc.gpsimd.tensor_tensor(rstd2[:, t:t + 1], var2[:, t:t + 1], minus_half[:, 0:1], ALU.pow).then_inc(rstd2_ready, 1)

            ctx_low(0)
            xT_low(0)
            power1(0)

            def body(b, first, last):
                for t in range(LT):
                    power2(b, t)
                if not last:
                    ctx_low(b + 1)
                    power1(b + 1)
                    xT_low(b + 1)

            over_batches(pool, body)


def kernel(**inputs):
    import numpy as np
    import concourse.bacc as bacc
    from concourse.bass_utils import run_bass_kernel_spmd

    def tiled(a, rows, cols):
        return np.ascontiguousarray(a.reshape(rows, P, cols).transpose(1, 0, 2))

    x = np.asarray(inputs["x"])
    ctx = np.asarray(inputs["ctx_1024"])
    B, L, D = x.shape
    C = ctx.shape[2]
    wq, wk = np.asarray(inputs["L0_xattn_Wq"]), np.asarray(inputs["L0_xattn_Wk"])
    wg = np.asarray(inputs["L0_ffn_W_gate"])
    arrays = {
        "x": np.stack([tiled(x[b], L // P, D) for b in range(B)]),
        "xT": np.stack([tiled(x[b].T, D // P, L) for b in range(B)]),
        "ctxT": np.stack([tiled(ctx[b].T, C // P, L) for b in range(B)]),
        "WqkT": np.ascontiguousarray(np.stack([tiled(wq.T, C // P, wq.shape[0]), tiled(wk.T, C // P, wk.shape[0])], axis=2)),
        "bqk": np.ascontiguousarray(np.stack([np.asarray(inputs["L0_xattn_bq"]), np.asarray(inputs["L0_xattn_bk"])], axis=1)),
        "WupT": tiled(np.asarray(inputs["L0_ffn_W_up"]).T, D // P, D),
        "WdownT": tiled(np.asarray(inputs["L0_ffn_W_down"]).T, D // P, D),
        "Wexpert": tiled(np.asarray(inputs["L0_ffn_W_expert"]), D // P, D),
        "WgateT": tiled(wg.T, D // P, wg.shape[0]),
    }
    nc = bacc.Bacc("TRN2", target_bir_lowering=False, num_devices=1)
    args = [nc.dram_tensor(f"in_{name}", a.shape, mybir.dt.from_np(a.dtype), kind="ExternalInput").ap()
            for name, a in arrays.items()]
    args.append(nc.dram_tensor("out", (B, P, L // P, D), F32, kind="ExternalOutput").ap())
    build(nc, *args)
    r = run_bass_kernel_spmd(nc, [{f"in_{name}": a for name, a in arrays.items()}], core_ids=[0])
    got = np.asarray(r.results[0]["out"]).reshape(B, P, L // P, D)
    return np.ascontiguousarray(got.transpose(0, 2, 1, 3)).reshape(B, L, D)
```

```python
from contextlib import ExitStack

import concourse.bass as bass
from concourse import mybir

ALU = mybir.AluOpType
ACT = mybir.ActivationFunctionType
AX = mybir.AxisListType
F32 = mybir.dt.float32
PART = mybir.dt.float16

P = 128
W_SCALE = 2.0**4

EPS = 1e-5


def build(nc, x, xT, ctxT, WqkT, bqk, WupT, WdownT, Wexpert, WgateT, out):
    B, _, LT, D = x.shape
    KT = D // P
    L = LT * P
    CT = ctxT.shape[2]
    H = WqkT.shape[3]
    E = WgateT.shape[2]
    A_SCALE = float(D)
    assert D == L and H == P and E == 8

    es = ExitStack()

    def sb(name, shape, dt=F32):
        return es.enter_context(nc.sbuf_tensor(name, shape, dt))

    def bank(name):
        return es.enter_context(nc.psum_tensor(name, [P, 512], F32))

    def sem(name):
        return es.enter_context(nc.semaphore(name))

    with es:
        x_sb = sb("x_sb", [P, LT, D])
        xT_sb = sb("xT_sb", [P, KT, L])
        xT_hi = sb("xT_hi", [P, KT, L], PART)
        xT_lo = sb("xT_lo", [P, KT, L], PART)
        ctx_sb = sb("ctx_sb", [P, CT, L])
        ctx_hi = sb("ctx_hi", [P, CT, L], PART)
        ctx_lo = sb("ctx_lo", [P, CT, L], PART)
        qk_hi = sb("qk_hi", [P, 2, L], PART)
        qk_lo = sb("qk_lo", [P, 2, L], PART)
        attn = sb("attn", [P, KT, D])
        attnT_hi = sb("attnT_hi", [P, KT, D], PART)
        attnT_lo = sb("attnT_lo", [P, KT, D], PART)
        x2 = sb("x2", [P, LT, D])
        y = sb("y", [P, LT, D])
        yT_hi = sb("yT_hi", [P, KT, L], PART)
        yT_lo = sb("yT_lo", [P, KT, L], PART)
        hT_hi = sb("hT_hi", [P, KT, L], PART)
        hT_lo = sb("hT_lo", [P, KT, L], PART)
        base = sb("base", [P, LT, D])
        out_sb = sb("out_sb", [P, LT, D])

        wqk = sb("wqk", [P, CT, 2, H])
        wqk_hi = sb("wqk_hi", [P, CT, 2, H], PART)
        wqk_lo = sb("wqk_lo", [P, CT, 2, H], PART)
        bias = sb("bias", [P, 2])
        bias_scaled = sb("bias_scaled", [P, 2])
        wgate = sb("wgate", [P, KT, E])
        wgate_hl = sb("wgate_hl", [P, KT, 2, E], PART)
        wexp = sb("wexp", [P, KT, D])
        wexp_hi = sb("wexp_hi", [P, KT, D], PART)
        wexp_lo = sb("wexp_lo", [P, KT, D], PART)
        wup = sb("wup", [P, KT, D])
        wup_hi = sb("wup_hi", [P, KT, D], PART)
        wup_lo = sb("wup_lo", [P, KT, D], PART)
        wdown = sb("wdown", [P, KT, D])
        wdown_hi = sb("wdown_hi", [P, KT, D], PART)
        wdown_lo = sb("wdown_lo", [P, KT, D], PART)

        identity = sb("identity", [P, P])
        zeros = sb("zeros", [P, 512], PART)
        minus_one = sb("minus_one", [P, 1])
        minus_half = sb("minus_half", [P, LT])
        neg_max = sb("neg_max", [P, KT])
        row_max = sb("row_max", [P, KT])
        row_sum = sb("row_sum", [P, KT])
        row_mean = sb("row_mean", [P, KT])
        row_inv = sb("row_inv", [P, KT])
        stats1 = sb("stats1", [P, LT, 6])
        mean_var1 = sb("mean_var1", [P, LT, 2])
        var1 = sb("var1", [P, LT])
        rstd1 = sb("rstd1", [P, LT])
        stats2 = sb("stats2", [P, LT, 6])
        mean_var2 = sb("mean_var2", [P, LT, 2])
        mean2 = sb("mean2", [P, LT])
        var2 = sb("var2", [P, LT])
        rstd2 = sb("rstd2", [P, LT])
        logits = sb("logits", [P, LT, E])
        top = sb("top", [P, LT, 8])
        top_one = sb("top_one", [P, LT])
        neg_top = sb("neg_top", [P, LT])
        top_exp = sb("top_exp", [P, LT, 2])
        top_sum = sb("top_sum", [P, LT])
        top_inv = sb("top_inv", [P, LT])
        top_prob = sb("top_prob", [P, LT, 2])
        route = sb("route", [P, LT])

        small = [bank("small0"), bank("small1")]
        turned = [bank("turned0"), bank("turned1")]
        big = [bank(f"big{i}") for i in range(4)]

        ctx_in, x_in, xT_in = sem("ctx_in"), sem("x_in"), sem("xT_in")
        wqk_in, wexp_in, wup_in, wdown_in = sem("wqk_in"), sem("wexp_in"), sem("wup_in"), sem("wdown_in")
        out_stored, last_stored = sem("out_stored"), sem("last_stored")
        minus_one_ready = sem("minus_one_ready")
        identity_ready, zeros_ready = sem("identity_ready"), sem("zeros_ready")
        bias_in, bias_ready = sem("bias_in"), sem("bias_ready")
        wqk_hi_ready, wqk_split = sem("wqk_hi_ready"), sem("wqk_split")
        wexp_hi_ready, wexp_split = sem("wexp_hi_ready"), sem("wexp_split")
        wup_hi_ready, wup_split = sem("wup_hi_ready"), sem("wup_split")
        wdown_hi_ready, wdown_split = sem("wdown_hi_ready"), sem("wdown_split")
        ctx_hi_ready, ctx_split = sem("ctx_hi_ready"), sem("ctx_split")
        xT_hi_ready, xT_split = sem("xT_hi_ready"), sem("xT_split")
        proj_ready = sem("proj_ready")
        qk_hi_ready, qk_split = sem("qk_hi_ready"), sem("qk_split")
        energy_ready = sem("energy_ready")
        max_ready, neg_max_ready = sem("max_ready"), sem("neg_max_ready")
        exp_ready = sem("exp_ready")
        row_mean_ready, row_inv_ready = sem("row_mean_ready"), sem("row_inv_ready")
        attn_ready = sem("attn_ready")
        turned_ready, turned_hi_ready, turned_split = sem("turned_ready"), sem("turned_hi_ready"), sem("turned_split")
        stats1_ready, mean1_ready, var1_ready, rstd1_ready = (
            sem("stats1_ready"), sem("mean1_ready"), sem("var1_ready"), sem("rstd1_ready"))
        mix_ready = sem("mix_ready")
        x2_ready, stats2_ready, mean2_ready = sem("x2_ready"), sem("stats2_ready"), sem("mean2_ready")
        var2_ready, rstd2_ready, y_ready = sem("var2_ready"), sem("rstd2_ready"), sem("y_ready")
        gate_ready, logits_ready, top_ready, neg_top_ready = (
            sem("gate_ready"), sem("logits_ready"), sem("top_ready"), sem("neg_top_ready"))
        top_exp_ready, top_inv_ready, top_prob_ready, route_ready = (
            sem("top_exp_ready"), sem("top_inv_ready"), sem("top_prob_ready"), sem("route_ready"))
        expert_ready, base_ready = sem("expert_ready"), sem("base_ready")
        up_ready, hT_hi_ready, hT_split = sem("up_ready"), sem("hT_hi_ready"), sem("hT_split")
        down_ready, out_ready = sem("down_ready"), sem("out_ready")

        def energy_bank(b, m):
            return big[m] if isinstance(b, int) and b == 0 else small[m % 2]

        def expert_bank(t, last):
            return small[0] if last and t == LT - 1 else big[t]

        block = es.enter_context(nc.Block())

        def over_batches(eng, body):
            body(0, True, False)
            with eng.Fori(1, B - 1) as b:
                body(b, False, False)
            body(B - 1, False, True)

        @block.sync
        def _(sp):
            def load_ctx(b):
                sp.wait_ge(ctx_split, b * CT)
                sp.dma_start(ctx_sb[:], ctxT[b]).then_inc(ctx_in, 16)

            sp.dma_start(ctx_sb[:], ctxT[0]).then_inc(ctx_in, 16)
            sp.dma_start(wqk[:], WqkT).then_inc(wqk_in, 16)
            sp.dma_start(bias[:], bqk).then_inc(bias_in, 16)
            sp.dma_start(x_sb[:], x[0]).then_inc(x_in, 16)
            sp.dma_start(xT_sb[:], xT[0]).then_inc(xT_in, 16)
            load_ctx(1)
            sp.dma_start(wexp[:], Wexpert).then_inc(wexp_in, 16)
            sp.dma_start(wgate[:], WgateT).then_inc(wexp_in, 16)
            sp.dma_start(wup[:], WupT).then_inc(wup_in, 16)
            sp.dma_start(wdown[:], WdownT).then_inc(wdown_in, 16)

            def body(b, first, last):
                if not last:
                    if not first:
                        load_ctx(b + 1)
                    sp.wait_ge(xT_split, b + 1)
                    sp.dma_start(xT_sb[:], xT[b + 1]).then_inc(xT_in, 16)
                    sp.wait_ge(x2_ready, b * LT + LT)
                    sp.dma_start(x_sb[:], x[b + 1]).then_inc(x_in, 16)
                else:
                    for t in range(LT):
                        sp.wait_ge(out_ready, b * LT + t + 1)
                        sp.dma_start(out[b, :, t, :], out_sb[:, t, :]).then_inc(last_stored, 16)

            over_batches(sp, body)
            sp.wait_ge(out_stored, (B - 1) * 16)
            sp.wait_ge(last_stored, LT * 16)

        @block.tensor
        def _(pe):
            def product(bank_out, lhs_hi, lhs_lo, rhs_hi, rhs_lo, n, before_last=None):
                for k in range(n):
                    if before_last and k == n - 1:
                        pe.wait_ge(*before_last)
                    pe.matmul(bank_out, lhs_hi(k), rhs_hi(k), start=(k == 0), stop=False)
                    pe.matmul(bank_out, lhs_hi(k), rhs_lo(k), start=False, stop=False)
                    mm = pe.matmul(bank_out, lhs_lo(k), rhs_hi(k), start=False, stop=(k == n - 1))
                return mm

            def project(b):
                pe.wait_ge(ctx_split, b * CT + CT)
                for i in range(2):
                    product(small[1 - i][:], lambda c: wqk_hi[:, c, i, :], lambda c: wqk_lo[:, c, i, :],
                            lambda c: ctx_hi[:, c, :], lambda c: ctx_lo[:, c, :], CT).then_inc(proj_ready, 1)

            def energies(b, tiles):
                for m in tiles:
                    if m == 0:
                        pe.wait_ge(qk_split, b * 2 + 2)
                    if m >= 2 and energy_bank(b, m) is small[m % 2]:
                        pe.wait_ge(exp_ready, b * KT + m - 1)
                    rows = slice(m * P, m * P + P)
                    product(energy_bank(b, m)[:], lambda k: qk_hi[:, 0, rows], lambda k: qk_lo[:, 0, rows],
                            lambda k: qk_hi[:, 1, :], lambda k: qk_lo[:, 1, :], 1).then_inc(energy_ready, 1)

            def turn(n, src):
                for k in range(KT):
                    mm = pe.transpose(turned[n % 2][:, k * P:(k + 1) * P], src[:, k * P:(k + 1) * P], identity[:])
                mm.then_inc(turned_ready, 1)

            def turn_attn(b, tiles, first=False):
                for m in tiles:
                    if m >= 2 or not first:
                        pe.wait_ge(turned_split, b * (KT + LT) + m - 1)
                    pe.wait_ge(attn_ready, b * KT + m + 1)
                    turn(m, attn[:, m, :])

            def turn_y(b, t):
                pe.wait_ge(turned_split, b * (KT + LT) + KT + t - 1)
                pe.wait_ge(y_ready, b * LT + t + 1)
                turn(KT + t, y[:, t, :])

            def mix(b, t, first):
                if t == 0:
                    pe.wait_ge(turned_split, b * (KT + LT) + KT)
                    pe.wait_ge(xT_split, b + 1)
                if not first:
                    pe.wait_ge(out_ready, b * LT + t + 1 - LT)
                rows = slice(t * P, t * P + P)
                product(big[t][:], lambda k: xT_hi[:, k, rows], lambda k: xT_lo[:, k, rows],
                        lambda k: attnT_hi[:, k, :], lambda k: attnT_lo[:, k, :], KT).then_inc(mix_ready, 1)

            def expert(b, t, first, last):
                if first and t == 0:
                    pe.wait_ge(wexp_split, 3)
                if first and t < 2:
                    pe.wait_ge(qk_split, 4 - t)
                pe.wait_ge(turned_split, b * (KT + LT) + KT + t + 1)
                if t >= 2:
                    pe.wait_ge(logits_ready, b * LT + t - 1)
                rows = slice(t * P, t * P + P)
                g = small[t % 2][:, 0:2 * E]
                for k in range(KT):
                    pe.matmul(g, yT_hi[:, k, rows], wgate_hl[:, k, :, :].rearrange("p a e -> p (a e)"),
                              start=(k == 0), stop=False)
                    mm = pe.matmul(g[:, 0:E], yT_lo[:, k, rows], wgate_hl[:, k, 0, :],
                                   start=False, stop=(k == KT - 1))
                mm.then_inc(gate_ready, 1)
                if expert_bank(t, last) is big[t]:
                    pe.wait_ge(x2_ready, b * LT + t + 1)
                else:
                    pe.wait_ge(logits_ready, b * LT + t)
                product(expert_bank(t, last)[:], lambda k: yT_hi[:, k, rows], lambda k: yT_lo[:, k, rows],
                        lambda k: wexp_hi[:, k, :], lambda k: wexp_lo[:, k, :], KT).then_inc(expert_ready, 1)

            def up(b, f, first, last):
                if first and f == 0:
                    pe.wait_ge(wup_split, 1)
                if expert_bank(f, last) is big[f]:
                    pe.wait_ge(base_ready, b * LT + f + 1)
                else:
                    pe.wait_ge(x2_ready, b * LT + f + 1)
                rows = slice(f * P, f * P + P)
                product(big[f][:], lambda k: wup_hi[:, k, rows], lambda k: wup_lo[:, k, rows],
                        lambda k: yT_hi[:, k, :], lambda k: yT_lo[:, k, :], KT).then_inc(up_ready, 1)

            def down(b, t, first):
                if first and t == 0:
                    pe.wait_ge(wdown_split, 1)
                if t == 0:
                    pe.wait_ge(hT_split, b * KT + KT - 1)
                rows = slice(t * P, t * P + P)
                product(big[t][:], lambda k: hT_hi[:, k, rows], lambda k: hT_lo[:, k, rows],
                        lambda k: wdown_hi[:, k, :], lambda k: wdown_lo[:, k, :], KT,
                        before_last=(hT_split, b * KT + KT) if t == 0 else None).then_inc(down_ready, 1)

            def keep_warm(bank_out, n):
                for _ in range(n):
                    pe.matmul(bank_out[:], zeros[:, 0:P], zeros[:], start=True, stop=True)

            pe.wait_ge(zeros_ready, 1)
            keep_warm(turned[0], 11)
            pe.wait_ge(wqk_split, 1)
            project(0)
            keep_warm(turned[0], 5)
            energies(0, range(KT))
            keep_warm(turned[1], 8)
            pe.wait_ge(identity_ready, 2)
            turn_attn(0, (0,), first=True)
            project(1)
            turn_attn(0, (1, 2, 3), first=True)

            def body(b, first, last):
                mix(b, 0, first)
                mix(b, 1, first)
                mix(b, 2, first)
                turn_y(b, 0)
                mix(b, 3, first)
                turn_y(b, 1)
                expert(b, 0, first, last)
                turn_y(b, 2)
                expert(b, 1, first, last)
                turn_y(b, 3)
                expert(b, 2, first, last)
                if not last:
                    expert(b, 3, first, last)
                    pe.wait_ge(logits_ready, b * LT + LT)
                    if not first:
                        project(b + 1)
                else:
                    pe.wait_ge(turned_split, b * (KT + LT) + KT + LT)
                up(b, 0, first, last)
                up(b, 1, first, last)
                up(b, 2, first, last)
                if not last:
                    energies(b + 1, (0, 1))
                up(b, 3, first, last)
                if not last:
                    energies(b + 1, (2, 3))
                else:
                    expert(b, 3, first, last)
                down(b, 0, first)
                down(b, 1, first)
                if not last:
                    turn_attn(b + 1, (0, 1))
                down(b, 2, first)
                if not last:
                    turn_attn(b + 1, (2, 3))
                down(b, 3, first)

            over_batches(pe, body)

        @block.scalar
        def _(act):
            def ctx_high(b):
                act.wait_ge(ctx_in, b * 16 + 16)
                act.wait_ge(proj_ready, b * 2)
                nc.scalar.copy(ctx_hi[:], ctx_sb[:]).then_inc(ctx_hi_ready, 1)

            def xT_high(b):
                act.wait_ge(xT_in, b * 16 + 16)
                nc.scalar.copy(xT_hi[:], xT_sb[:]).then_inc(xT_hi_ready, 1)

            def qk_high(b):
                for i in range(2):
                    act.wait_ge(proj_ready, b * 2 + i + 1)
                    nc.scalar.activation(qk_hi[:, i, :], small[1 - i][:], ACT.Identity,
                                         bias=bias_scaled[:, i:i + 1]).then_inc(qk_hi_ready, 1)

            def exps(b, tiles):
                for m in tiles:
                    act.wait_ge(neg_max_ready, b * KT + m + 1)
                    nc.scalar.activation(attn[:, m, :], energy_bank(b, m)[:], ACT.Exp, bias=neg_max[:, m:m + 1],
                                         scale=1 / W_SCALE**2, accum_out=row_sum[:, m:m + 1]).then_inc(exp_ready, 1)

            def normalize(b, m):
                act.wait_ge(row_inv_ready, b * KT + m + 1)
                nc.scalar.activation(attn[:, m, :], attn[:, m, :], ACT.Identity, bias=minus_one[:, 0:1],
                                     scale=row_inv[:, m:m + 1]).then_inc(attn_ready, 1)

            def turned_high(b, n, to, t):
                act.wait_ge(turned_ready, b * (KT + LT) + n + 1)
                nc.scalar.copy(to[:, :, t * P:(t + 1) * P],
                               turned[n % 2][:].rearrange("p (k c) -> p k c", k=KT)).then_inc(turned_hi_ready, 1)

            def gate_exp(b, t):
                act.wait_ge(neg_top_ready, b * LT + t + 1)
                nc.scalar.activation(top_exp[:, t, :], top[:, t, 0:2], ACT.Exp, bias=neg_top[:, t:t + 1],
                                     scale=1 / W_SCALE, accum_out=top_sum[:, t:t + 1]).then_inc(top_exp_ready, 1)

            def relu_high(b, f):
                act.wait_ge(up_ready, b * KT + f + 1)
                nc.scalar.activation(hT_hi[:, f, :], big[f][:], ACT.Relu).then_inc(hT_hi_ready, 1)

            def weight_scale(arrived, n, w, ready):
                act.wait_ge(arrived, n)
                nc.scalar.mul(w, w, W_SCALE).then_inc(ready, 1)

            def weight_high(hi, w, ready, n):
                act.wait_ge(ready, n)
                nc.scalar.copy(hi, w).then_inc(ready, 1)

            act.wait_ge(wqk_in, 16)
            nc.scalar.mul(wqk_hi[:], wqk[:], W_SCALE).then_inc(wqk_hi_ready, 1)
            act.wait_ge(bias_in, 16)
            nc.scalar.mul(bias_scaled[:], bias[:], W_SCALE).then_inc(bias_ready, 1)
            act.wait_ge(bias_ready, 1)
            qk_high(0)
            xT_high(0)
            ctx_high(1)
            act.wait_ge(minus_one_ready, 1)
            exps(0, (0, 1))
            normalize(0, 0)
            exps(0, (2, 3))
            turned_high(0, 0, attnT_hi, 0)
            normalize(0, 1)
            normalize(0, 2)
            turned_high(0, 1, attnT_hi, 1)
            normalize(0, 3)
            turned_high(0, 2, attnT_hi, 2)
            turned_high(0, 3, attnT_hi, 3)
            qk_high(1)
            weight_scale(wexp_in, 32, wgate[:], wexp_hi_ready)
            weight_scale(wexp_in, 32, wexp[:], wexp_hi_ready)
            weight_high(wgate_hl[:, :, 0, :], wgate[:], wexp_hi_ready, 2)
            weight_high(wexp_hi[:], wexp[:], wexp_hi_ready, 2)

            def body(b, first, last):
                if first:
                    weight_scale(wup_in, 16, wup[:], wup_hi_ready)
                    weight_high(wup_hi[:], wup[:], wup_hi_ready, 1)
                else:
                    act.wait_ge(out_ready, b * LT)
                    act.dma_start(out[b - 1].rearrange("p t n -> p (t n)"),
                                  out_sb[:].rearrange("p t n -> p (t n)")).then_inc(out_stored, 16)
                if not first and not last:
                    ctx_high(b + 1)
                turned_high(b, KT + 0, yT_hi, 0)
                turned_high(b, KT + 1, yT_hi, 1)
                turned_high(b, KT + 2, yT_hi, 2)
                gate_exp(b, 0)
                turned_high(b, KT + 3, yT_hi, 3)
                if first:
                    weight_scale(wdown_in, 16, wdown[:], wdown_hi_ready)
                gate_exp(b, 1)
                gate_exp(b, 2)
                if first:
                    weight_high(wdown_hi[:], wdown[:], wdown_hi_ready, 1)
                if not last:
                    gate_exp(b, 3)
                if not first and not last:
                    qk_high(b + 1)
                relu_high(b, 0)
                if not last:
                    xT_high(b + 1)
                relu_high(b, 1)
                relu_high(b, 2)
                if not last:
                    exps(b + 1, (0, 1))
                relu_high(b, 3)
                if last:
                    gate_exp(b, 3)
                if not last:
                    exps(b + 1, (2,))
                    normalize(b + 1, 0)
                    exps(b + 1, (3,))
                    for m in range(1, KT):
                        normalize(b + 1, m)
                    for m in range(KT):
                        turned_high(b + 1, m, attnT_hi, m)

            over_batches(act, body)

        @block.vector
        def _(dve):
            def qk_low(b, which=(0, 1)):
                for i in which:
                    dve.wait_ge(qk_hi_ready, b * 2 + i + 1)
                    nc.vector.scalar_tensor_tensor(out=qk_lo[:, i, :], in0=small[1 - i][:], scalar=bias_scaled[:, i:i + 1],
                                                   in1=qk_hi[:, i, :], op0=ALU.add, op1=ALU.subtract).then_inc(qk_split, 1)

            def maxima(b, tiles):
                for m in tiles:
                    dve.wait_ge(energy_ready, b * KT + m + 1)
                    nc.vector.tensor_reduce(row_max[:, m:m + 1], energy_bank(b, m)[:], AX.X, ALU.max).then_inc(max_ready, 1)
                    dve.wait_ge(max_ready, b * KT + m + 1)
                    nc.vector.tensor_scalar(neg_max[:, m:m + 1], row_max[:, m:m + 1], -1 / W_SCALE**2, None,
                                            ALU.mult).then_inc(neg_max_ready, 1)

            def inverse_means(b, tiles):
                for m in tiles:
                    dve.wait_ge(exp_ready, b * KT + m + 1)
                    nc.vector.tensor_scalar(row_mean[:, m:m + 1], row_sum[:, m:m + 1], 1.0 / D, None,
                                            ALU.mult).then_inc(row_mean_ready, 1)
                    dve.wait_ge(row_mean_ready, b * KT + m + 1)
                    nc.vector.reciprocal(row_inv[:, m:m + 1], row_mean[:, m:m + 1]).then_inc(row_inv_ready, 1)

            def turned_low(b, n, hi, lo, t):
                dve.wait_ge(turned_hi_ready, b * (KT + LT) + n + 1)
                cols = slice(t * P, (t + 1) * P)
                nc.vector.tensor_tensor(lo[:, :, cols], turned[n % 2][:].rearrange("p (k c) -> p k c", k=KT),
                                        hi[:, :, cols], ALU.subtract).then_inc(turned_split, 1)

            def statistics1(b, t):
                if t == 0:
                    dve.wait_ge(x_in, b * 16 + 16)
                else:
                    dve.wait_ge(stats1_ready, b * LT + t)
                nc.vector.bn_stats(stats1[:, t, :], x_sb[:, t, :]).then_inc(stats1_ready, 1)
                if t > 0:
                    nc.vector.bn_aggr(mean_var1[:, t - 1, :], stats1[:, t - 1, :]).then_inc(mean1_ready, 1)

            def variance1(b):
                dve.wait_ge(stats1_ready, b * LT + LT)
                dve.wait_ge(mean1_ready, b * LT + LT - 1)
                nc.vector.tensor_scalar(var1[:, 0:LT - 1], mean_var1[:, 0:LT - 1, 1], EPS, A_SCALE**2,
                                        ALU.add, ALU.mult).then_inc(var1_ready, 1)
                nc.vector.bn_aggr(mean_var1[:, LT - 1, :], stats1[:, LT - 1, :]).then_inc(mean1_ready, 1)
                dve.wait_ge(mean1_ready, b * LT + LT)
                nc.vector.tensor_scalar(var1[:, LT - 1:LT], mean_var1[:, LT - 1, 1:2], EPS, A_SCALE**2,
                                        ALU.add, ALU.mult).then_inc(var1_ready, 1)

            def residual(b, t):
                dve.wait_ge(mix_ready, b * LT + t + 1)
                if t == 0:
                    dve.wait_ge(rstd1_ready, b + 1)
                nc.vector.scalar_tensor_tensor(out=x2[:, t, :], in0=big[t][:], scalar=rstd1[:, t:t + 1], in1=x_sb[:, t, :],
                                               op0=ALU.mult, op1=ALU.add).then_inc(x2_ready, 1)
                dve.wait_ge(x2_ready, b * LT + t + 1)
                nc.vector.bn_stats(stats2[:, t, :], x2[:, t, :]).then_inc(stats2_ready, 1)
                dve.wait_ge(stats2_ready, b * LT + t + 1)
                nc.vector.tensor_scalar(mean2[:, t:t + 1], stats2[:, t, 1:2], stats2[:, t, 4:5], 0.5,
                                        ALU.add, ALU.mult).then_inc(mean2_ready, 1)
                nc.vector.bn_aggr(mean_var2[:, t, :], stats2[:, t, :]).then_inc(mean2_ready, 1)
                dve.wait_ge(mean2_ready, (b * LT + t + 1) * 2)
                nc.vector.tensor_scalar(var2[:, t:t + 1], mean_var2[:, t, 1:2], EPS, None, ALU.add).then_inc(var2_ready, 1)

            def norm_y(b, t):
                dve.wait_ge(rstd2_ready, b * LT + t + 1)
                nc.vector.tensor_scalar(y[:, t, :], x2[:, t, :], mean2[:, t:t + 1], rstd2[:, t:t + 1],
                                        ALU.subtract, ALU.mult).then_inc(y_ready, 1)

            def gate(b, t):
                dve.wait_ge(gate_ready, b * LT + t + 1)
                nc.vector.tensor_reduce(logits[:, t, :], small[t % 2][:, 0:2 * E].rearrange("p (a e) -> p e a", a=2),
                                        AX.X, ALU.add).then_inc(logits_ready, 1)
                dve.wait_ge(logits_ready, b * LT + t + 1)
                nc.vector.tensor_reduce(top_one[:, t:t + 1], logits[:, t, :], AX.X, ALU.max).then_inc(top_ready, 1)
                nc.vector.max(top[:, t, :], logits[:, t, :]).then_inc(top_ready, 1)
                dve.wait_ge(top_ready, (b * LT + t + 1) * 2)
                nc.vector.tensor_scalar(neg_top[:, t:t + 1], top_one[:, t:t + 1], -1 / W_SCALE, None,
                                        ALU.mult).then_inc(neg_top_ready, 1)

            def routed(b, t, last):
                dve.wait_ge(top_exp_ready, b * LT + t + 1)
                nc.vector.reciprocal(top_inv[:, t:t + 1], top_sum[:, t:t + 1]).then_inc(top_inv_ready, 1)
                dve.wait_ge(top_inv_ready, b * LT + t + 1)
                nc.vector.tensor_scalar(top_prob[:, t, :], top_exp[:, t, :], top_inv[:, t:t + 1], 1 / W_SCALE,
                                        ALU.mult, ALU.mult).then_inc(top_prob_ready, 1)
                dve.wait_ge(top_prob_ready, b * LT + t + 1)
                nc.vector.tensor_reduce(route[:, t:t + 1], top_prob[:, t, :], AX.X, ALU.add).then_inc(route_ready, 1)
                dve.wait_ge(route_ready, b * LT + t + 1)
                dve.wait_ge(expert_ready, b * LT + t + 1)
                nc.vector.scalar_tensor_tensor(out=base[:, t, :], in0=expert_bank(t, last)[:], scalar=route[:, t:t + 1], in1=x2[:, t, :],
                                               op0=ALU.mult, op1=ALU.add).then_inc(base_ready, 1)

            def relu_low(b, f):
                dve.wait_ge(hT_hi_ready, b * KT + f + 1)
                nc.vector.scalar_tensor_tensor(out=hT_lo[:, f, :], in0=big[f][:], scalar=0.0, in1=hT_hi[:, f, :],
                                               op0=ALU.max, op1=ALU.subtract).then_inc(hT_split, 1)

            def finish(b, t):
                dve.wait_ge(down_ready, b * LT + t + 1)
                dve.wait_ge(base_ready, b * LT + t + 1)
                if not isinstance(b, int) or b > 0:
                    dve.wait_ge(out_stored, b * 16)
                nc.vector.scalar_tensor_tensor(out=out_sb[:, t, :], in0=big[t][:], scalar=1 / W_SCALE**2, in1=base[:, t, :],
                                               op0=ALU.mult, op1=ALU.add).then_inc(out_ready, 1)

            nc.vector.memset(zeros[:], 0.0).then_inc(zeros_ready, 1)
            nc.vector.memset(minus_one[:], -1.0).then_inc(minus_one_ready, 1)
            dve.wait_ge(ctx_in, 16)
            nc.vector.tensor_copy(ctx_hi[:], ctx_sb[:]).then_inc(ctx_hi_ready, 1)
            dve.wait_ge(ctx_hi_ready, 1)
            nc.vector.tensor_tensor(ctx_lo[:, 0, :], ctx_sb[:, 0, :], ctx_hi[:, 0, :], ALU.subtract).then_inc(ctx_split, 1)
            dve.wait_ge(wqk_hi_ready, 1)
            nc.vector.scalar_tensor_tensor(out=wqk_lo[:], in0=wqk[:], scalar=W_SCALE, in1=wqk_hi[:],
                                           op0=ALU.mult, op1=ALU.subtract).then_inc(wqk_split, 1)
            dve.wait_ge(bias_ready, 1)
            qk_low(0, (0,))
            statistics1(0, 0)
            qk_low(0, (1,))
            statistics1(0, 1)
            maxima(0, (0, 1))
            inverse_means(0, (0,))
            maxima(0, (2, 3))
            inverse_means(0, (1, 2, 3))
            for m in range(KT):
                turned_low(0, m, attnT_hi, attnT_lo, m)
            statistics1(0, 2)
            statistics1(0, 3)
            variance1(0)
            qk_low(1)

            def body(b, first, last):
                residual(b, 0)
                residual(b, 1)
                norm_y(b, 0)
                residual(b, 2)
                norm_y(b, 1)
                turned_low(b, KT + 0, yT_hi, yT_lo, 0)
                residual(b, 3)
                norm_y(b, 2)
                turned_low(b, KT + 1, yT_hi, yT_lo, 1)
                norm_y(b, 3)
                gate(b, 0)
                turned_low(b, KT + 2, yT_hi, yT_lo, 2)
                gate(b, 1)
                routed(b, 0, last)
                turned_low(b, KT + 3, yT_hi, yT_lo, 3)
                gate(b, 2)
                routed(b, 1, last)
                routed(b, 2, last)
                if not last:
                    gate(b, 3)
                    routed(b, 3, last)
                if not first and not last:
                    qk_low(b + 1)
                relu_low(b, 0)
                if not last:
                    for t in range(LT):
                        statistics1(b + 1, t)
                    variance1(b + 1)
                relu_low(b, 1)
                relu_low(b, 2)
                if not last:
                    maxima(b + 1, (0, 1))
                relu_low(b, 3)
                if not last:
                    maxima(b + 1, (2,))
                    inverse_means(b + 1, (0,))
                    maxima(b + 1, (3,))
                    inverse_means(b + 1, (1, 2, 3))
                else:
                    gate(b, 3)
                    routed(b, 3, last)
                finish(b, 0)
                finish(b, 1)
                if not last:
                    turned_low(b + 1, 0, attnT_hi, attnT_lo, 0)
                    turned_low(b + 1, 1, attnT_hi, attnT_lo, 1)
                finish(b, 2)
                if not last:
                    turned_low(b + 1, 2, attnT_hi, attnT_lo, 2)
                    turned_low(b + 1, 3, attnT_hi, attnT_lo, 3)
                finish(b, 3)

            over_batches(dve, body)

        @block.gpsimd
        def _(pool):
            nc.gpsimd.memset(identity[:], 0.0).then_inc(identity_ready, 1)
            pool.wait_ge(identity_ready, 1)
            nc.gpsimd.affine_select(out=identity[:], in_=identity[:], compare_op=ALU.not_equal, fill=1.0, base=0,
                                    pattern=[[-1, P]], channel_multiplier=1).then_inc(identity_ready, 1)
            nc.gpsimd.memset(minus_half[:], -0.5).then_inc(identity_ready, 1)
            pool.wait_ge(identity_ready, 3)

            def ctx_low(b, tiles):
                pool.wait_ge(ctx_hi_ready, b + 1)
                for c in tiles:
                    nc.gpsimd.tensor_tensor(ctx_lo[:, c, :], ctx_sb[:, c, :], ctx_hi[:, c, :],
                                            ALU.subtract).then_inc(ctx_split, 1)

            def weight_low(hi_ready, n, lo, w, hi, ready):
                pool.wait_ge(hi_ready, n)
                nc.gpsimd.tensor_tensor(lo, w, hi, ALU.subtract).then_inc(ready, 1)

            def xT_low(b):
                pool.wait_ge(xT_hi_ready, b + 1)
                nc.gpsimd.tensor_tensor(xT_lo[:], xT_sb[:], xT_hi[:], ALU.subtract).then_inc(xT_split, 1)

            def power1(b):
                pool.wait_ge(var1_ready, b * 2 + 2)
                nc.gpsimd.tensor_tensor(rstd1[:], var1[:], minus_half[:], ALU.pow).then_inc(rstd1_ready, 1)

            def power2(b, t):
                pool.wait_ge(var2_ready, b * LT + t + 1)
                nc.gpsimd.tensor_tensor(rstd2[:, t:t + 1], var2[:, t:t + 1], minus_half[:, 0:1], ALU.pow).then_inc(rstd2_ready, 1)

            ctx_low(0, range(1, CT))
            ctx_low(1, range(CT))
            xT_low(0)
            power1(0)
            weight_low(wexp_hi_ready, 4, wgate_hl[:, :, 1, :], wgate[:], wgate_hl[:, :, 0, :], wexp_split)

            def body(b, first, last):
                for t in range(LT):
                    if first and t < 2:
                        half = slice(t * KT // 2, (t + 1) * KT // 2)
                        weight_low(wexp_hi_ready, 4, wexp_lo[:, half, :], wexp[:, half, :], wexp_hi[:, half, :], wexp_split)
                    power2(b, t)
                if not first and not last:
                    ctx_low(b + 1, range(CT))
                if first:
                    weight_low(wup_hi_ready, 2, wup_lo[:], wup[:], wup_hi[:], wup_split)
                if first:
                    weight_low(wdown_hi_ready, 2, wdown_lo[:], wdown[:], wdown_hi[:], wdown_split)
                if not last:
                    power1(b + 1)
                    xT_low(b + 1)

            over_batches(pool, body)


def kernel(**inputs):
    import numpy as np
    import concourse.bacc as bacc
    from concourse.bass_utils import run_bass_kernel_spmd

    def tiled(a, rows, cols):
        return np.ascontiguousarray(a.reshape(rows, P, cols).transpose(1, 0, 2))

    x = np.asarray(inputs["x"])
    ctx = np.asarray(inputs["ctx_1024"])
    B, L, D = x.shape
    C = ctx.shape[2]
    wq, wk = np.asarray(inputs["L0_xattn_Wq"]), np.asarray(inputs["L0_xattn_Wk"])
    wg = np.asarray(inputs["L0_ffn_W_gate"])
    arrays = {
        "x": np.stack([tiled(x[b], L // P, D) for b in range(B)]),
        "xT": np.stack([tiled(x[b].T, D // P, L) for b in range(B)]),
        "ctxT": np.stack([tiled(ctx[b].T, C // P, L) for b in range(B)]),
        "WqkT": np.ascontiguousarray(np.stack([tiled(wq.T, C // P, wq.shape[0]), tiled(wk.T, C // P, wk.shape[0])], axis=2)),
        "bqk": np.ascontiguousarray(np.stack([np.asarray(inputs["L0_xattn_bq"]), np.asarray(inputs["L0_xattn_bk"])], axis=1)),
        "WupT": tiled(np.asarray(inputs["L0_ffn_W_up"]).T, D // P, D),
        "WdownT": tiled(np.asarray(inputs["L0_ffn_W_down"]).T, D // P, D),
        "Wexpert": tiled(np.asarray(inputs["L0_ffn_W_expert"]), D // P, D),
        "WgateT": tiled(wg.T, D // P, wg.shape[0]),
    }
    nc = bacc.Bacc("TRN2", target_bir_lowering=False, num_devices=1)
    args = [nc.dram_tensor(f"in_{name}", a.shape, mybir.dt.from_np(a.dtype), kind="ExternalInput").ap()
            for name, a in arrays.items()]
    args.append(nc.dram_tensor("out", (B, P, L // P, D), F32, kind="ExternalOutput").ap())
    build(nc, *args)
    r = run_bass_kernel_spmd(nc, [{f"in_{name}": a for name, a in arrays.items()}], core_ids=[0])
    got = np.asarray(r.results[0]["out"]).reshape(B, P, L // P, D)
    return np.ascontiguousarray(got.transpose(0, 2, 1, 3)).reshape(B, L, D)
```

```python
from contextlib import ExitStack

from concourse import mybir

ALU = mybir.AluOpType
ACT = mybir.ActivationFunctionType
AX = mybir.AxisListType
F32 = mybir.dt.float32
PART = mybir.dt.float16

P = 128
W_SCALE = 2.0**4

EPS = 1e-5


def build(nc, x, xT, ctxT, WqkT, bqk, WupT, WdownT, Wexpert, WgateT, out):
    B, _, LT, D = x.shape
    KT = D // P
    L = LT * P
    CT = ctxT.shape[2]
    H = WqkT.shape[3]
    E = WgateT.shape[2]
    A_SCALE = float(D)
    assert D == L and H == P and E == 8

    es = ExitStack()

    def sb(name, shape, dt=F32):
        return es.enter_context(nc.sbuf_tensor(name, shape, dt))

    def bank(name):
        return es.enter_context(nc.psum_tensor(name, [P, 512], F32))

    def sem(name):
        return es.enter_context(nc.semaphore(name))

    with es:
        x_sb = sb("x_sb", [P, LT, D])
        xT_sb = sb("xT_sb", [P, KT, L])
        xT_hi = sb("xT_hi", [P, KT, L], PART)
        xT_lo = sb("xT_lo", [P, KT, L], PART)
        ctx_sb = sb("ctx_sb", [P, CT, L])
        ctx_hi = sb("ctx_hi", [P, CT, L], PART)
        ctx_lo = sb("ctx_lo", [P, CT, L], PART)
        qk_hi = sb("qk_hi", [P, 2, L], PART)
        qk_lo = sb("qk_lo", [P, 2, L], PART)
        attn = sb("attn", [P, KT, D])
        attnT_hi = sb("attnT_hi", [P, KT, D], PART)
        attnT_lo = sb("attnT_lo", [P, KT, D], PART)
        x2 = sb("x2", [P, LT, D])
        y = sb("y", [P, LT, D])
        yT_hi = sb("yT_hi", [P, KT, L], PART)
        yT_lo = sb("yT_lo", [P, KT, L], PART)
        hT_hi = sb("hT_hi", [P, KT, L], PART)
        hT_lo = sb("hT_lo", [P, KT, L], PART)
        base = sb("base", [P, LT, D])
        out_sb = sb("out_sb", [P, LT, D])

        wqk = sb("wqk", [P, CT, 2, H])
        wqk_hi = sb("wqk_hi", [P, CT, 2, H], PART)
        wqk_lo = sb("wqk_lo", [P, CT, 2, H], PART)
        bias = sb("bias", [P, 2])
        bias_scaled = sb("bias_scaled", [P, 2])
        wgate = sb("wgate", [P, KT, E])
        wgate_hl = sb("wgate_hl", [P, KT, 2, E], PART)
        wexp = sb("wexp", [P, KT, D])
        wexp_hi = sb("wexp_hi", [P, KT, D], PART)
        wexp_lo = sb("wexp_lo", [P, KT, D], PART)
        wup = sb("wup", [P, KT, D])
        wup_hi = sb("wup_hi", [P, KT, D], PART)
        wup_lo = sb("wup_lo", [P, KT, D], PART)
        wdown = sb("wdown", [P, KT, D])
        wdown_hi = sb("wdown_hi", [P, KT, D], PART)
        wdown_lo = sb("wdown_lo", [P, KT, D], PART)

        identity = sb("identity", [P, P])
        zeros = sb("zeros", [P, 512], PART)
        minus_mean = sb("minus_mean", [P, 1])
        minus_half = sb("minus_half", [P, LT])
        neg_max = sb("neg_max", [P, KT])
        row_max = sb("row_max", [P, KT])
        row_sum = sb("row_sum", [P, KT])
        row_inv = sb("row_inv", [P, KT])
        stats1 = sb("stats1", [P, LT, 6])
        mean_var1 = sb("mean_var1", [P, LT, 2])
        var1 = sb("var1", [P, LT])
        rstd1 = sb("rstd1", [P, LT])
        stats2 = sb("stats2", [P, LT, 6])
        mean_var2 = sb("mean_var2", [P, LT, 2])
        mean2 = sb("mean2", [P, LT])
        var2 = sb("var2", [P, LT])
        rstd2 = sb("rstd2", [P, LT])
        logits = sb("logits", [P, LT, E])
        top = sb("top", [P, LT, 8])
        top_one = sb("top_one", [P, LT])
        neg_top = sb("neg_top", [P, LT])
        top_exp = sb("top_exp", [P, LT, 2])
        top_sum = sb("top_sum", [P, LT])
        top_inv = sb("top_inv", [P, LT])
        top_prob = sb("top_prob", [P, LT, 2])
        route = sb("route", [P, LT])

        small = [bank("small0"), bank("small1")]
        turned = [bank("turned0"), bank("turned1")]
        big = [bank(f"big{i}") for i in range(4)]

        ctx_in, x_in, xT_in = sem("ctx_in"), sem("x_in"), sem("xT_in")
        wqk_in, wexp_in, wup_in, wdown_in = sem("wqk_in"), sem("wexp_in"), sem("wup_in"), sem("wdown_in")
        out_stored, last_stored = sem("out_stored"), sem("last_stored")
        minus_mean_ready = sem("minus_mean_ready")
        identity_ready, zeros_ready = sem("identity_ready"), sem("zeros_ready")
        bias_in, bias_ready = sem("bias_in"), sem("bias_ready")
        wqk_hi_ready, wqk_split = sem("wqk_hi_ready"), sem("wqk_split")
        wexp_hi_ready, wexp_split = sem("wexp_hi_ready"), sem("wexp_split")
        wup_hi_ready, wup_split = sem("wup_hi_ready"), sem("wup_split")
        wdown_hi_ready, wdown_split = sem("wdown_hi_ready"), sem("wdown_split")
        ctx_hi_ready, ctx_split = sem("ctx_hi_ready"), sem("ctx_split")
        xT_hi_ready, xT_split = sem("xT_hi_ready"), sem("xT_split")
        proj_ready = sem("proj_ready")
        qk_hi_ready, qk_split = sem("qk_hi_ready"), sem("qk_split")
        energy_ready = sem("energy_ready")
        max_ready, neg_max_ready = sem("max_ready"), sem("neg_max_ready")
        exp_ready = sem("exp_ready")
        row_inv_ready = sem("row_inv_ready")
        attn_ready = sem("attn_ready")
        turned_ready, turned_hi_ready, turned_split = sem("turned_ready"), sem("turned_hi_ready"), sem("turned_split")
        stats1_ready, mean1_ready, var1_ready, rstd1_ready = (
            sem("stats1_ready"), sem("mean1_ready"), sem("var1_ready"), sem("rstd1_ready"))
        mix_ready = sem("mix_ready")
        x2_ready, stats2_ready, mean2_ready = sem("x2_ready"), sem("stats2_ready"), sem("mean2_ready")
        var2_ready, rstd2_ready, y_ready = sem("var2_ready"), sem("rstd2_ready"), sem("y_ready")
        gate_ready, logits_ready, top_ready, neg_top_ready = (
            sem("gate_ready"), sem("logits_ready"), sem("top_ready"), sem("neg_top_ready"))
        top_exp_ready, top_inv_ready, top_prob_ready, route_ready = (
            sem("top_exp_ready"), sem("top_inv_ready"), sem("top_prob_ready"), sem("route_ready"))
        expert_ready, base_ready = sem("expert_ready"), sem("base_ready")
        up_ready, hT_hi_ready, hT_split = sem("up_ready"), sem("hT_hi_ready"), sem("hT_split")
        down_ready, out_ready = sem("down_ready"), sem("out_ready")

        def proj_bank(b, i):
            return small[i] if isinstance(b, int) and b == 1 else small[1 - i]

        def energy_bank(b, m):
            return big[m] if isinstance(b, int) and b == 0 else small[m % 2]

        def expert_bank(t, last):
            return small[0] if last and t == LT - 1 else big[t]

        def down_parts(t, last):
            if last and t == LT - 1:
                return (slice(0, D // 2), big[t]), (slice(D // 2, D), turned[0])
            return ((slice(0, D), big[t]),)

        halves = (slice(0, KT // 2), slice(KT // 2, KT))

        block = es.enter_context(nc.Block())

        def over_batches(eng, body):
            body(0, True, False)
            with eng.Fori(1, B - 1) as b:
                body(b, False, False)
            body(B - 1, False, True)

        @block.sync
        def _(sp):
            def load_ctx(b):
                sp.wait_ge(ctx_split, b * CT)
                sp.dma_start(ctx_sb[:], ctxT[b]).then_inc(ctx_in, 16)

            sp.dma_start(ctx_sb[:], ctxT[0]).then_inc(ctx_in, 16)
            sp.dma_start(wqk[:], WqkT).then_inc(wqk_in, 16)
            sp.dma_start(bias[:], bqk).then_inc(bias_in, 16)
            sp.dma_start(x_sb[:], x[0]).then_inc(x_in, 16)
            sp.dma_start(xT_sb[:], xT[0]).then_inc(xT_in, 16)
            load_ctx(1)
            sp.dma_start(wexp[:], Wexpert).then_inc(wexp_in, 16)
            sp.dma_start(wgate[:], WgateT).then_inc(wexp_in, 16)
            sp.dma_start(wup[:], WupT).then_inc(wup_in, 16)
            sp.dma_start(wdown[:], WdownT).then_inc(wdown_in, 16)

            def body(b, first, last):
                if not last:
                    if not first:
                        load_ctx(b + 1)
                    sp.wait_ge(xT_split, b * 2 + 2)
                    sp.dma_start(xT_sb[:], xT[b + 1]).then_inc(xT_in, 16)
                    sp.wait_ge(x2_ready, b * LT + LT)
                    sp.dma_start(x_sb[:], x[b + 1]).then_inc(x_in, 16)
                else:
                    for t in range(LT):
                        for h, (cols, _) in enumerate(down_parts(t, last)):
                            sp.wait_ge(out_ready, b * LT + t + h + 1)
                            sp.dma_start(out[b, :, t, cols], out_sb[:, t, cols]).then_inc(last_stored, 16)

            over_batches(sp, body)
            sp.wait_ge(out_stored, (B - 1) * 16)
            sp.wait_ge(last_stored, (LT + 1) * 16)

        @block.tensor
        def _(pe):
            def product(bank_out, lhs_hi, lhs_lo, rhs_hi, rhs_lo, n, before_last=None):
                for k in range(n):
                    if before_last and k == n - 1:
                        pe.wait_ge(*before_last)
                    pe.matmul(bank_out, lhs_hi(k), rhs_hi(k), start=(k == 0), stop=False)
                    pe.matmul(bank_out, lhs_hi(k), rhs_lo(k), start=False, stop=False)
                    mm = pe.matmul(bank_out, lhs_lo(k), rhs_hi(k), start=False, stop=(k == n - 1))
                return mm

            def project(b, which=(0, 1)):
                pe.wait_ge(ctx_split, b * CT + CT)
                for i in which:
                    product(proj_bank(b, i)[:], lambda c: wqk_hi[:, c, i, :], lambda c: wqk_lo[:, c, i, :],
                            lambda c: ctx_hi[:, c, :], lambda c: ctx_lo[:, c, :], CT).then_inc(proj_ready, 1)

            def energies(b, tiles):
                for m in tiles:
                    if m == 0:
                        pe.wait_ge(qk_split, b * 2 + 2)
                    if m >= 2:
                        pe.wait_ge(exp_ready, b * KT + m - 1)
                    rows = slice(m * P, m * P + P)
                    product(energy_bank(b, m)[:], lambda k: qk_hi[:, 0, rows], lambda k: qk_lo[:, 0, rows],
                            lambda k: qk_hi[:, 1, :], lambda k: qk_lo[:, 1, :], 1).then_inc(energy_ready, 1)

            def project_first():
                pe.wait_ge(ctx_hi_ready, 1)
                pe.wait_ge(wqk_hi_ready, 1)
                for i in range(2):
                    for c in range(CT):
                        pe.matmul(proj_bank(0, i)[:], wqk_hi[:, c, i, :], ctx_hi[:, c, :], start=(c == 0), stop=False)
                pe.wait_ge(ctx_split, CT)
                pe.wait_ge(wqk_split, 1)
                for i in range(2):
                    for c in range(CT):
                        pe.matmul(proj_bank(0, i)[:], wqk_hi[:, c, i, :], ctx_lo[:, c, :], start=False, stop=False)
                        mm = pe.matmul(proj_bank(0, i)[:], wqk_lo[:, c, i, :], ctx_hi[:, c, :],
                                       start=False, stop=(c == CT - 1))
                    mm.then_inc(proj_ready, 1)

            def energies_first():
                pe.wait_ge(qk_hi_ready, 2)
                for m in range(KT):
                    rows = slice(m * P, m * P + P)
                    pe.matmul(energy_bank(0, m)[:], qk_hi[:, 0, rows], qk_hi[:, 1, :], start=True, stop=False)
                pe.wait_ge(qk_split, 2)
                for m in range(KT):
                    rows = slice(m * P, m * P + P)
                    pe.matmul(energy_bank(0, m)[:], qk_hi[:, 0, rows], qk_lo[:, 1, :], start=False, stop=False)
                    pe.matmul(energy_bank(0, m)[:], qk_lo[:, 0, rows], qk_hi[:, 1, :],
                              start=False, stop=True).then_inc(energy_ready, 1)

            def turn(n, src):
                for k in range(KT):
                    mm = pe.transpose(turned[n % 2][:, k * P:(k + 1) * P], src[:, k * P:(k + 1) * P], identity[:])
                mm.then_inc(turned_ready, 1)

            def turn_attn(b, tiles, first=False):
                for m in tiles:
                    if m >= 2 or not first:
                        pe.wait_ge(turned_split, b * (KT + LT) + m - 1)
                    pe.wait_ge(attn_ready, b * KT + m + 1)
                    turn(m, attn[:, m, :])

            def turn_y(b, t):
                pe.wait_ge(turned_split, b * (KT + LT) + KT + t - 1)
                pe.wait_ge(y_ready, b * LT + t + 1)
                turn(KT + t, y[:, t, :])

            def mix_product(t, cols):
                rows = slice(t * P, t * P + P)
                return product(big[t][:, cols], lambda k: xT_hi[:, k, rows], lambda k: xT_lo[:, k, rows],
                               lambda k: attnT_hi[:, k, cols], lambda k: attnT_lo[:, k, cols], KT)

            def mix(b, t, first):
                if t == 0:
                    pe.wait_ge(turned_split, b * (KT + LT) + KT)
                    if not first:
                        pe.wait_ge(xT_split, b * 2 + 2)
                if not first:
                    pe.wait_ge(out_ready, b * LT + t + 1 - LT)
                mix_product(t, slice(2 * P, D) if first else slice(0, D)).then_inc(mix_ready, 1)

            def expert(b, t, first, last):
                if first and t == 0:
                    pe.wait_ge(wexp_split, KT)
                if first and t < 2:
                    pe.wait_ge(qk_split, 3 + t)
                pe.wait_ge(turned_split, b * (KT + LT) + KT + t + 1)
                if t >= 2:
                    pe.wait_ge(logits_ready, b * LT + t - 1)
                rows = slice(t * P, t * P + P)
                g = small[t % 2][:, 0:2 * E]
                for k in range(KT):
                    pe.matmul(g, yT_hi[:, k, rows], wgate_hl[:, k, :, :].rearrange("p a e -> p (a e)"),
                              start=(k == 0), stop=False)
                    mm = pe.matmul(g[:, 0:E], yT_lo[:, k, rows], wgate_hl[:, k, 0, :],
                                   start=False, stop=(k == KT - 1))
                mm.then_inc(gate_ready, 1)
                if expert_bank(t, last) is big[t]:
                    pe.wait_ge(x2_ready, b * LT + t + 1)
                else:
                    pe.wait_ge(logits_ready, b * LT + t)
                product(expert_bank(t, last)[:], lambda k: yT_hi[:, k, rows], lambda k: yT_lo[:, k, rows],
                        lambda k: wexp_hi[:, k, :], lambda k: wexp_lo[:, k, :], KT,
                        before_last=(wexp_split, 1 + KT) if first and t == 0 else None).then_inc(expert_ready, 1)

            def up(b, f, first, last):
                if first and f == 0:
                    pe.wait_ge(wup_split, 1)
                if expert_bank(f, last) is big[f]:
                    pe.wait_ge(base_ready, b * LT + f + 1)
                else:
                    pe.wait_ge(x2_ready, b * LT + f + 1)
                rows = slice(f * P, f * P + P)
                product(big[f][:], lambda k: wup_hi[:, k, rows], lambda k: wup_lo[:, k, rows],
                        lambda k: yT_hi[:, k, :], lambda k: yT_lo[:, k, :], KT).then_inc(up_ready, 1)

            def down(b, t, first, last):
                if first and t == 0:
                    pe.wait_ge(wdown_split, 1)
                if t == 0:
                    pe.wait_ge(hT_split, b * KT + KT - 1)
                rows = slice(t * P, t * P + P)
                for cols, to in down_parts(t, last):
                    product(to[:, cols], lambda k: hT_hi[:, k, rows], lambda k: hT_lo[:, k, rows],
                            lambda k: wdown_hi[:, k, cols], lambda k: wdown_lo[:, k, cols], KT,
                            before_last=(hT_split, b * KT + KT) if t == 0 else None).then_inc(down_ready, 1)

            def keep_warm(bank_out, n):
                for _ in range(n):
                    pe.matmul(bank_out[:], zeros[:, 0:P], zeros[:], start=True, stop=True)

            pe.wait_ge(zeros_ready, 1)
            keep_warm(turned[0], 10)
            project_first()
            keep_warm(turned[0], 4)
            energies_first()
            keep_warm(turned[1], 6)
            pe.wait_ge(identity_ready, 2)
            turn_attn(0, (0,), first=True)
            keep_warm(small[0], 6)
            pe.wait_ge(turned_split, 1)
            pe.wait_ge(xT_split, 2)
            for t in range(LT):
                pe.wait_ge(exp_ready, t + 1)
                mix_product(t, slice(0, P))
                if t == 0:
                    turn_attn(0, (1,), first=True)
            turn_attn(0, (2,), first=True)
            pe.wait_ge(turned_split, 2)
            for t in range(LT):
                mix_product(t, slice(P, 2 * P))
                if t == 0:
                    turn_attn(0, (3,), first=True)

            def body(b, first, last):
                mix(b, 0, first)
                mix(b, 1, first)
                mix(b, 2, first)
                if first:
                    project(1, (0,))
                turn_y(b, 0)
                mix(b, 3, first)
                if first:
                    project(1, (1,))
                turn_y(b, 1)
                expert(b, 0, first, last)
                turn_y(b, 2)
                expert(b, 1, first, last)
                turn_y(b, 3)
                expert(b, 2, first, last)
                if not last:
                    expert(b, 3, first, last)
                    pe.wait_ge(logits_ready, b * LT + LT)
                    if not first:
                        project(b + 1)
                else:
                    pe.wait_ge(turned_split, b * (KT + LT) + KT + LT)
                up(b, 0, first, last)
                up(b, 1, first, last)
                up(b, 2, first, last)
                if not last:
                    energies(b + 1, (0, 1))
                up(b, 3, first, last)
                if not last:
                    energies(b + 1, (2, 3))
                else:
                    expert(b, 3, first, last)
                down(b, 0, first, last)
                down(b, 1, first, last)
                if not last:
                    turn_attn(b + 1, (0, 1))
                down(b, 2, first, last)
                if not last:
                    turn_attn(b + 1, (2, 3))
                down(b, 3, first, last)

            over_batches(pe, body)

        @block.scalar
        def _(act):
            def ctx_high(b):
                act.wait_ge(ctx_in, b * 16 + 16)
                act.wait_ge(proj_ready, b * 2)
                nc.scalar.copy(ctx_hi[:], ctx_sb[:]).then_inc(ctx_hi_ready, 1)

            def xT_high(b, halves):
                act.wait_ge(xT_in, b * 16 + 16)
                for half in halves:
                    nc.scalar.copy(xT_hi[:, half, :], xT_sb[:, half, :]).then_inc(xT_hi_ready, 1)

            def qk_high(b, which=(0, 1)):
                for i in which:
                    act.wait_ge(proj_ready, b * 2 + i + 1)
                    nc.scalar.activation(qk_hi[:, i, :], proj_bank(b, i)[:], ACT.Identity,
                                         bias=bias_scaled[:, i:i + 1]).then_inc(qk_hi_ready, 1)

            def exps(b, tiles):
                for m in tiles:
                    act.wait_ge(neg_max_ready, b * KT + m + 1)
                    nc.scalar.activation(attn[:, m, :], energy_bank(b, m)[:], ACT.Exp, bias=neg_max[:, m:m + 1],
                                         scale=1 / W_SCALE**2, accum_out=row_sum[:, m:m + 1]).then_inc(exp_ready, 1)

            def normalize(b, m):
                act.wait_ge(row_inv_ready, b * KT + m + 1)
                nc.scalar.activation(attn[:, m, :], attn[:, m, :], ACT.Identity, bias=minus_mean[:, 0:1],
                                     scale=row_inv[:, m:m + 1]).then_inc(attn_ready, 1)

            def turned_high(b, n, to, t):
                act.wait_ge(turned_ready, b * (KT + LT) + n + 1)
                nc.scalar.mul(to[:, :, t * P:(t + 1) * P], turned[n % 2][:].rearrange("p (k c) -> p k c", k=KT),
                              A_SCALE if n < KT else 1.0).then_inc(turned_hi_ready, 1)

            def gate_exp(b, t):
                act.wait_ge(neg_top_ready, b * LT + t + 1)
                nc.scalar.activation(top_exp[:, t, :], top[:, t, 0:2], ACT.Exp, bias=neg_top[:, t:t + 1],
                                     scale=1 / W_SCALE, accum_out=top_sum[:, t:t + 1]).then_inc(top_exp_ready, 1)

            def relu_high(b, f):
                act.wait_ge(up_ready, b * KT + f + 1)
                nc.scalar.activation(hT_hi[:, f, :], big[f][:], ACT.Relu).then_inc(hT_hi_ready, 1)

            def weight_scale(arrived, n, w, ready):
                act.wait_ge(arrived, n)
                nc.scalar.mul(w, w, W_SCALE).then_inc(ready, 1)

            def weight_high(hi, w, ready, n):
                act.wait_ge(ready, n)
                nc.scalar.copy(hi, w).then_inc(ready, 1)

            act.wait_ge(wqk_in, 16)
            nc.scalar.mul(wqk_hi[:], wqk[:], W_SCALE).then_inc(wqk_hi_ready, 1)
            act.wait_ge(bias_in, 16)
            nc.scalar.mul(bias_scaled[:], bias[:], W_SCALE).then_inc(bias_ready, 1)
            act.wait_ge(bias_ready, 1)
            qk_high(0)
            xT_high(0, halves[:1])
            act.wait_ge(minus_mean_ready, 1)
            exps(0, (0,))
            normalize(0, 0)
            exps(0, (1,))
            turned_high(0, 0, attnT_hi, 0)
            normalize(0, 1)
            exps(0, (2, 3))
            turned_high(0, 1, attnT_hi, 1)
            normalize(0, 2)
            normalize(0, 3)
            turned_high(0, 2, attnT_hi, 2)
            turned_high(0, 3, attnT_hi, 3)
            ctx_high(1)
            weight_scale(wexp_in, 32, wgate[:], wexp_hi_ready)
            weight_scale(wexp_in, 32, wexp[:], wexp_hi_ready)
            weight_high(wgate_hl[:, :, 0, :], wgate[:], wexp_hi_ready, 2)
            weight_high(wexp_hi[:], wexp[:], wexp_hi_ready, 2)
            qk_high(1, (0,))

            def body(b, first, last):
                if not first:
                    act.wait_ge(out_ready, b * LT)
                    act.dma_start(out[b - 1].rearrange("p t n -> p (t n)"),
                                  out_sb[:].rearrange("p t n -> p (t n)")).then_inc(out_stored, 16)
                if not first and not last:
                    ctx_high(b + 1)
                turned_high(b, KT + 0, yT_hi, 0)
                if first:
                    weight_scale(wup_in, 16, wup[:], wup_hi_ready)
                    qk_high(1, (1,))
                turned_high(b, KT + 1, yT_hi, 1)
                if first:
                    weight_high(wup_hi[:], wup[:], wup_hi_ready, 1)
                turned_high(b, KT + 2, yT_hi, 2)
                gate_exp(b, 0)
                turned_high(b, KT + 3, yT_hi, 3)
                if first:
                    weight_scale(wdown_in, 16, wdown[:], wdown_hi_ready)
                gate_exp(b, 1)
                gate_exp(b, 2)
                if first:
                    weight_high(wdown_hi[:], wdown[:], wdown_hi_ready, 1)
                if not last:
                    gate_exp(b, 3)
                if not first and not last:
                    qk_high(b + 1)
                relu_high(b, 0)
                if not last:
                    xT_high(b + 1, halves)
                relu_high(b, 1)
                relu_high(b, 2)
                if not last:
                    exps(b + 1, (0, 1))
                relu_high(b, 3)
                if last:
                    gate_exp(b, 3)
                if not last:
                    exps(b + 1, (2,))
                    normalize(b + 1, 0)
                    exps(b + 1, (3,))
                    for m in range(1, KT):
                        normalize(b + 1, m)
                    for m in range(KT):
                        turned_high(b + 1, m, attnT_hi, m)

            over_batches(act, body)

        @block.vector
        def _(dve):
            def qk_low(b, which=(0, 1)):
                for i in which:
                    dve.wait_ge(qk_hi_ready, b * 2 + i + 1)
                    nc.vector.scalar_tensor_tensor(out=qk_lo[:, i, :], in0=proj_bank(b, i)[:], scalar=bias_scaled[:, i:i + 1],
                                                   in1=qk_hi[:, i, :], op0=ALU.add, op1=ALU.subtract).then_inc(qk_split, 1)

            def maxima(b, tiles):
                for m in tiles:
                    dve.wait_ge(energy_ready, b * KT + m + 1)
                    nc.vector.tensor_reduce(row_max[:, m:m + 1], energy_bank(b, m)[:], AX.X, ALU.max).then_inc(max_ready, 1)
                    dve.wait_ge(max_ready, b * KT + m + 1)
                    nc.vector.tensor_scalar(neg_max[:, m:m + 1], row_max[:, m:m + 1], -1 / W_SCALE**2, None,
                                            ALU.mult).then_inc(neg_max_ready, 1)

            def inverse_sums(b, tiles):
                for m in tiles:
                    dve.wait_ge(exp_ready, b * KT + m + 1)
                    nc.vector.reciprocal(row_inv[:, m:m + 1], row_sum[:, m:m + 1]).then_inc(row_inv_ready, 1)

            def turned_low(b, n, hi, lo, t):
                dve.wait_ge(turned_hi_ready, b * (KT + LT) + n + 1)
                cols = slice(t * P, (t + 1) * P)
                blocks = turned[n % 2][:].rearrange("p (k c) -> p k c", k=KT)
                if n < KT:
                    nc.vector.scalar_tensor_tensor(out=lo[:, :, cols], in0=blocks, scalar=A_SCALE, in1=hi[:, :, cols],
                                                   op0=ALU.mult, op1=ALU.subtract).then_inc(turned_split, 1)
                else:
                    nc.vector.tensor_tensor(lo[:, :, cols], blocks, hi[:, :, cols], ALU.subtract).then_inc(turned_split, 1)

            def statistics1(b, t):
                if t == 0:
                    dve.wait_ge(x_in, b * 16 + 16)
                else:
                    dve.wait_ge(stats1_ready, b * LT + t)
                nc.vector.bn_stats(stats1[:, t, :], x_sb[:, t, :]).then_inc(stats1_ready, 1)
                if t > 0:
                    nc.vector.bn_aggr(mean_var1[:, t - 1, :], stats1[:, t - 1, :]).then_inc(mean1_ready, 1)

            def variance1(b):
                dve.wait_ge(stats1_ready, b * LT + LT)
                dve.wait_ge(mean1_ready, b * LT + LT - 1)
                nc.vector.tensor_scalar(var1[:, 0:LT - 1], mean_var1[:, 0:LT - 1, 1], EPS, A_SCALE**2,
                                        ALU.add, ALU.mult).then_inc(var1_ready, 1)
                nc.vector.bn_aggr(mean_var1[:, LT - 1, :], stats1[:, LT - 1, :]).then_inc(mean1_ready, 1)
                dve.wait_ge(mean1_ready, b * LT + LT)
                nc.vector.tensor_scalar(var1[:, LT - 1:LT], mean_var1[:, LT - 1, 1:2], EPS, A_SCALE**2,
                                        ALU.add, ALU.mult).then_inc(var1_ready, 1)

            def residual(b, t):
                dve.wait_ge(mix_ready, b * LT + t + 1)
                if t == 0:
                    dve.wait_ge(rstd1_ready, b + 1)
                nc.vector.scalar_tensor_tensor(out=x2[:, t, :], in0=big[t][:], scalar=rstd1[:, t:t + 1], in1=x_sb[:, t, :],
                                               op0=ALU.mult, op1=ALU.add).then_inc(x2_ready, 1)
                dve.wait_ge(x2_ready, b * LT + t + 1)
                nc.vector.bn_stats(stats2[:, t, :], x2[:, t, :]).then_inc(stats2_ready, 1)
                dve.wait_ge(stats2_ready, b * LT + t + 1)
                nc.vector.tensor_scalar(mean2[:, t:t + 1], stats2[:, t, 1:2], stats2[:, t, 4:5], 0.5,
                                        ALU.add, ALU.mult).then_inc(mean2_ready, 1)
                nc.vector.bn_aggr(mean_var2[:, t, :], stats2[:, t, :]).then_inc(mean2_ready, 1)
                dve.wait_ge(mean2_ready, (b * LT + t + 1) * 2)
                nc.vector.tensor_scalar(var2[:, t:t + 1], mean_var2[:, t, 1:2], EPS, None, ALU.add).then_inc(var2_ready, 1)

            def norm_y(b, t):
                dve.wait_ge(rstd2_ready, b * LT + t + 1)
                nc.vector.tensor_scalar(y[:, t, :], x2[:, t, :], mean2[:, t:t + 1], rstd2[:, t:t + 1],
                                        ALU.subtract, ALU.mult).then_inc(y_ready, 1)

            def gate(b, t):
                dve.wait_ge(gate_ready, b * LT + t + 1)
                nc.vector.tensor_reduce(logits[:, t, :], small[t % 2][:, 0:2 * E].rearrange("p (a e) -> p e a", a=2),
                                        AX.X, ALU.add).then_inc(logits_ready, 1)
                dve.wait_ge(logits_ready, b * LT + t + 1)
                nc.vector.tensor_reduce(top_one[:, t:t + 1], logits[:, t, :], AX.X, ALU.max).then_inc(top_ready, 1)
                nc.vector.max(top[:, t, :], logits[:, t, :]).then_inc(top_ready, 1)
                dve.wait_ge(top_ready, (b * LT + t + 1) * 2)
                nc.vector.tensor_scalar(neg_top[:, t:t + 1], top_one[:, t:t + 1], -1 / W_SCALE, None,
                                        ALU.mult).then_inc(neg_top_ready, 1)

            def routed(b, t, last):
                dve.wait_ge(top_exp_ready, b * LT + t + 1)
                nc.vector.reciprocal(top_inv[:, t:t + 1], top_sum[:, t:t + 1]).then_inc(top_inv_ready, 1)
                dve.wait_ge(top_inv_ready, b * LT + t + 1)
                nc.vector.tensor_scalar(top_prob[:, t, :], top_exp[:, t, :], top_inv[:, t:t + 1], 1 / W_SCALE,
                                        ALU.mult, ALU.mult).then_inc(top_prob_ready, 1)
                dve.wait_ge(top_prob_ready, b * LT + t + 1)
                nc.vector.tensor_reduce(route[:, t:t + 1], top_prob[:, t, :], AX.X, ALU.add).then_inc(route_ready, 1)
                dve.wait_ge(route_ready, b * LT + t + 1)
                dve.wait_ge(expert_ready, b * LT + t + 1)
                nc.vector.scalar_tensor_tensor(out=base[:, t, :], in0=expert_bank(t, last)[:], scalar=route[:, t:t + 1], in1=x2[:, t, :],
                                               op0=ALU.mult, op1=ALU.add).then_inc(base_ready, 1)

            def relu_low(b, f):
                dve.wait_ge(hT_hi_ready, b * KT + f + 1)
                nc.vector.scalar_tensor_tensor(out=hT_lo[:, f, :], in0=big[f][:], scalar=0.0, in1=hT_hi[:, f, :],
                                               op0=ALU.max, op1=ALU.subtract).then_inc(hT_split, 1)

            def finish(b, t, last):
                dve.wait_ge(base_ready, b * LT + t + 1)
                if not isinstance(b, int) or b > 0:
                    dve.wait_ge(out_stored, b * 16)
                for h, (cols, to) in enumerate(down_parts(t, last)):
                    dve.wait_ge(down_ready, b * LT + t + h + 1)
                    nc.vector.scalar_tensor_tensor(out=out_sb[:, t, cols], in0=to[:, cols], scalar=1 / W_SCALE**2,
                                                   in1=base[:, t, cols], op0=ALU.mult, op1=ALU.add).then_inc(out_ready, 1)

            nc.vector.memset(zeros[:], 0.0).then_inc(zeros_ready, 1)
            nc.vector.memset(minus_mean[:], -1.0 / D).then_inc(minus_mean_ready, 1)
            dve.wait_ge(ctx_in, 16)
            nc.vector.tensor_copy(ctx_hi[:], ctx_sb[:]).then_inc(ctx_hi_ready, 1)
            dve.wait_ge(ctx_hi_ready, 1)
            nc.vector.tensor_tensor(ctx_lo[:, 0, :], ctx_sb[:, 0, :], ctx_hi[:, 0, :], ALU.subtract).then_inc(ctx_split, 1)
            dve.wait_ge(wqk_hi_ready, 1)
            nc.vector.scalar_tensor_tensor(out=wqk_lo[:], in0=wqk[:], scalar=W_SCALE, in1=wqk_hi[:],
                                           op0=ALU.mult, op1=ALU.subtract).then_inc(wqk_split, 1)
            dve.wait_ge(bias_ready, 1)
            qk_low(0)
            dve.wait_ge(xT_in, 16)
            nc.vector.tensor_copy(xT_hi[:, halves[1], :], xT_sb[:, halves[1], :]).then_inc(xT_hi_ready, 1)
            maxima(0, (0, 1))
            inverse_sums(0, (0,))
            maxima(0, (2,))
            inverse_sums(0, (1,))
            turned_low(0, 0, attnT_hi, attnT_lo, 0)
            maxima(0, (3,))
            inverse_sums(0, (2, 3))
            turned_low(0, 1, attnT_hi, attnT_lo, 1)
            statistics1(0, 0)
            statistics1(0, 1)
            statistics1(0, 2)
            turned_low(0, 2, attnT_hi, attnT_lo, 2)
            statistics1(0, 3)
            turned_low(0, 3, attnT_hi, attnT_lo, 3)
            variance1(0)

            def body(b, first, last):
                if first:
                    residual(b, 0)
                    norm_y(b, 0)
                    residual(b, 1)
                    turned_low(b, KT + 0, yT_hi, yT_lo, 0)
                    norm_y(b, 1)
                    qk_low(1, (0,))
                    residual(b, 2)
                    turned_low(b, KT + 1, yT_hi, yT_lo, 1)
                    norm_y(b, 2)
                    qk_low(1, (1,))
                    residual(b, 3)
                    turned_low(b, KT + 2, yT_hi, yT_lo, 2)
                else:
                    residual(b, 0)
                    residual(b, 1)
                    norm_y(b, 0)
                    residual(b, 2)
                    norm_y(b, 1)
                    turned_low(b, KT + 0, yT_hi, yT_lo, 0)
                    residual(b, 3)
                    norm_y(b, 2)
                    turned_low(b, KT + 1, yT_hi, yT_lo, 1)
                norm_y(b, 3)
                gate(b, 0)
                if not first:
                    turned_low(b, KT + 2, yT_hi, yT_lo, 2)
                gate(b, 1)
                routed(b, 0, last)
                turned_low(b, KT + 3, yT_hi, yT_lo, 3)
                gate(b, 2)
                routed(b, 1, last)
                routed(b, 2, last)
                if not last:
                    gate(b, 3)
                    routed(b, 3, last)
                if not first and not last:
                    qk_low(b + 1)
                relu_low(b, 0)
                if not last:
                    for t in range(LT):
                        statistics1(b + 1, t)
                    variance1(b + 1)
                relu_low(b, 1)
                relu_low(b, 2)
                if not last:
                    maxima(b + 1, (0, 1))
                relu_low(b, 3)
                if not last:
                    maxima(b + 1, (2,))
                    inverse_sums(b + 1, (0,))
                    maxima(b + 1, (3,))
                    inverse_sums(b + 1, (1, 2, 3))
                else:
                    gate(b, 3)
                    routed(b, 3, last)
                finish(b, 0, last)
                finish(b, 1, last)
                if not last:
                    turned_low(b + 1, 0, attnT_hi, attnT_lo, 0)
                    turned_low(b + 1, 1, attnT_hi, attnT_lo, 1)
                finish(b, 2, last)
                if not last:
                    turned_low(b + 1, 2, attnT_hi, attnT_lo, 2)
                    turned_low(b + 1, 3, attnT_hi, attnT_lo, 3)
                finish(b, 3, last)

            over_batches(dve, body)

        @block.gpsimd
        def _(pool):
            nc.gpsimd.memset(identity[:], 0.0).then_inc(identity_ready, 1)
            pool.wait_ge(identity_ready, 1)
            nc.gpsimd.affine_select(out=identity[:], in_=identity[:], compare_op=ALU.not_equal, fill=1.0, base=0,
                                    pattern=[[-1, P]], channel_multiplier=1).then_inc(identity_ready, 1)
            nc.gpsimd.memset(minus_half[:], -0.5).then_inc(identity_ready, 1)
            pool.wait_ge(identity_ready, 3)

            def ctx_low(b, tiles):
                pool.wait_ge(ctx_hi_ready, b + 1)
                for c in tiles:
                    nc.gpsimd.tensor_tensor(ctx_lo[:, c, :], ctx_sb[:, c, :], ctx_hi[:, c, :],
                                            ALU.subtract).then_inc(ctx_split, 1)

            def weight_low(hi_ready, n, lo, w, hi, ready):
                pool.wait_ge(hi_ready, n)
                nc.gpsimd.tensor_tensor(lo, w, hi, ALU.subtract).then_inc(ready, 1)

            def xT_low(b):
                for h, half in enumerate(halves):
                    pool.wait_ge(xT_hi_ready, 2 if isinstance(b, int) and b == 0 else b * 2 + h + 1)
                    nc.gpsimd.tensor_tensor(xT_lo[:, half, :], xT_sb[:, half, :], xT_hi[:, half, :],
                                            ALU.subtract).then_inc(xT_split, 1)

            def power1(b):
                pool.wait_ge(var1_ready, b * 2 + 2)
                nc.gpsimd.tensor_tensor(rstd1[:], var1[:], minus_half[:], ALU.pow).then_inc(rstd1_ready, 1)

            def power2(b, t):
                pool.wait_ge(var2_ready, b * LT + t + 1)
                nc.gpsimd.tensor_tensor(rstd2[:, t:t + 1], var2[:, t:t + 1], minus_half[:, 0:1], ALU.pow).then_inc(rstd2_ready, 1)

            ctx_low(0, range(1, CT))
            xT_low(0)
            power1(0)
            ctx_low(1, range(CT))

            def body(b, first, last):
                for t in range(LT):
                    power2(b, t)
                    if first and t == 0:
                        weight_low(wexp_hi_ready, 4, wgate_hl[:, :, 1, :], wgate[:], wgate_hl[:, :, 0, :], wexp_split)
                    if first and t < 2:
                        for k in range(t * KT // 2, (t + 1) * KT // 2):
                            weight_low(wexp_hi_ready, 4, wexp_lo[:, k, :], wexp[:, k, :], wexp_hi[:, k, :], wexp_split)
                if not first and not last:
                    ctx_low(b + 1, range(CT))
                if first:
                    weight_low(wup_hi_ready, 2, wup_lo[:], wup[:], wup_hi[:], wup_split)
                    weight_low(wdown_hi_ready, 2, wdown_lo[:], wdown[:], wdown_hi[:], wdown_split)
                if not last:
                    power1(b + 1)
                    xT_low(b + 1)

            over_batches(pool, body)


def kernel(**inputs):
    import numpy as np
    import concourse.bacc as bacc
    from concourse.bass_utils import run_bass_kernel_spmd

    def tiled(a, rows, cols):
        return np.ascontiguousarray(a.reshape(rows, P, cols).transpose(1, 0, 2))

    x = np.asarray(inputs["x"])
    ctx = np.asarray(inputs["ctx_1024"])
    B, L, D = x.shape
    C = ctx.shape[2]
    wq, wk = np.asarray(inputs["L0_xattn_Wq"]), np.asarray(inputs["L0_xattn_Wk"])
    wg = np.asarray(inputs["L0_ffn_W_gate"])
    arrays = {
        "x": np.stack([tiled(x[b], L // P, D) for b in range(B)]),
        "xT": np.stack([tiled(x[b].T, D // P, L) for b in range(B)]),
        "ctxT": np.stack([tiled(ctx[b].T, C // P, L) for b in range(B)]),
        "WqkT": np.ascontiguousarray(np.stack([tiled(wq.T, C // P, wq.shape[0]), tiled(wk.T, C // P, wk.shape[0])], axis=2)),
        "bqk": np.ascontiguousarray(np.stack([np.asarray(inputs["L0_xattn_bq"]), np.asarray(inputs["L0_xattn_bk"])], axis=1)),
        "WupT": tiled(np.asarray(inputs["L0_ffn_W_up"]).T, D // P, D),
        "WdownT": tiled(np.asarray(inputs["L0_ffn_W_down"]).T, D // P, D),
        "Wexpert": tiled(np.asarray(inputs["L0_ffn_W_expert"]), D // P, D),
        "WgateT": tiled(wg.T, D // P, wg.shape[0]),
    }
    nc = bacc.Bacc("TRN2", target_bir_lowering=False, num_devices=1)
    args = [nc.dram_tensor(f"in_{name}", a.shape, mybir.dt.from_np(a.dtype), kind="ExternalInput").ap()
            for name, a in arrays.items()]
    args.append(nc.dram_tensor("out", (B, P, L // P, D), F32, kind="ExternalOutput").ap())
    build(nc, *args)
    r = run_bass_kernel_spmd(nc, [{f"in_{name}": a for name, a in arrays.items()}], core_ids=[0])
    got = np.asarray(r.results[0]["out"]).reshape(B, P, L // P, D)
    return np.ascontiguousarray(got.transpose(0, 2, 1, 3)).reshape(B, L, D)
```
